# Optimizing a Trainium2 kernel written in Bass

```python
import numpy as np
import jax
import jax.numpy as jnp

def _softmax(x, axis=-1):
    return jax.nn.softmax(x, axis=axis)

def _gelu(x):
    return jax.nn.gelu(x, approximate=True)

def _silu(x):
    return jax.nn.silu(x)

def _sigmoid(x):
    return jax.nn.sigmoid(x)

def _layernorm(x, axis=-1, eps=1e-05):
    m = jnp.mean(x, axis=axis, keepdims=True)
    v = jnp.var(x, axis=axis, keepdims=True)
    return (x - m) / jnp.sqrt(v + eps)

def _scatter_add(tgt, idx, src, axis=0):
    return tgt.at[idx].add(src)

def _segment_sum(src, seg, n):
    return jax.ops.segment_sum(src, seg, n)
kernel_name = 'mk_pixart_seq_d2_seqx_r4_a295e5'

def setup_inputs(seed: int=0):
    np.random.seed(seed)
    _w = jnp.asarray

    def _rec_inputs():
        import jax
        import jax.numpy as jnp
        _rk = jax.random.key(seed)
        x = 7.22e-05 + 1 * jax.random.normal(jax.random.fold_in(_rk, 1), (16, 256, 256), jnp.float32)
        _lenS = 256 - jax.random.randint(jax.random.fold_in(_rk, 7), (16,), 0, max(1, 256 // 4) + 1, jnp.int32)
        _lenS2 = 256 - jax.random.randint(jax.random.fold_in(_rk, 8), (16,), 0, max(1, 256 // 4) + 1, jnp.int32)
        cond_1024 = 0.000887014 + 1.03683 * jax.random.normal(jax.random.fold_in(_rk, 11), (16, 256), jnp.float32)
        _ctx_1024P = jax.random.normal(jax.random.fold_in(_rk, 12), (16, 16, 256), jnp.float32)
        _ctx_1024c = jax.random.dirichlet(jax.random.fold_in(_rk, 512), 0.3 * jnp.ones((16,), jnp.float32), (16, 256))
        _ctx_1024t = jnp.einsum('bsk,bkd->bsd', _ctx_1024c, _ctx_1024P)
        _ctx_1024t = _ctx_1024t * jax.lax.rsqrt(jnp.mean(jnp.square(_ctx_1024t)) + 1e-12) * 0.953939
        ctx_1024 = 0.00086875 + 0.999764 * (_ctx_1024t + 0.3 * jax.random.normal(jax.random.fold_in(_rk, 612), (16, 256, 256), jnp.float32))
        return (x, cond_1024, ctx_1024)
    x, cond_1024, ctx_1024 = _rec_inputs()

    def _L0_xcond_setup():
        import jax, jax.numpy as jnp
        import numpy as np
        C = 256
        H = 16
        D = C // H
        WIN = 128
        SHIFT = 64
        TOPK = 16
        HID = 1024
        EPS = 1e-06

        def _ln(x):
            x32 = x.astype(jnp.float32)
            m = x32.mean(-1, keepdims=True)
            v = jnp.mean((x32 - m) ** 2, axis=-1, keepdims=True)
            return ((x32 - m) * jax.lax.rsqrt(v + EPS)).astype(x.dtype)

        def _self_attn(h, w_qkv, b_qkv, w_so, b_so):
            B, L, _ = h.shape
            qkv = h @ w_qkv + b_qkv
            qkv = jnp.roll(qkv, -SHIFT, axis=1)
            nw = L // WIN
            qkv = qkv.reshape(B, nw, WIN, 3, H, D)
            q, k, v = (qkv[:, :, :, 0], qkv[:, :, :, 1], qkv[:, :, :, 2])
            scores = jnp.einsum('bnqhd,bnkhd->bnhqk', q, k) / jnp.sqrt(jnp.float32(D)).astype(h.dtype)
            attn = jax.nn.softmax(scores, axis=-1)
            o = jnp.einsum('bnhqk,bnkhd->bnqhd', attn, v).reshape(B, L, C)
            o = jnp.roll(o, SHIFT, axis=1)
            return o @ w_so + b_so

        def _topk_cross_attn(h, ctx, w_q, b_q, w_kv, b_kv, w_co, b_co):
            B, L, _ = h.shape
            Lc = ctx.shape[1]
            q = (h @ w_q + b_q).reshape(B, L, H, D)
            kv = (ctx @ w_kv + b_kv).reshape(B, Lc, 2, H, D)
            k, v = (kv[:, :, 0], kv[:, :, 1])
            scores = jnp.einsum('bqhd,bkhd->bhqk', q, k) / jnp.sqrt(jnp.float32(D)).astype(h.dtype)
            top_s, top_i = jax.lax.top_k(scores, TOPK)
            attn = jax.nn.softmax(top_s, axis=-1)
            v_bh = jnp.transpose(v, (0, 2, 1, 3))
            vg = jnp.take_along_axis(v_bh[:, :, None, :, :], top_i[..., None], axis=3)
            o = jnp.einsum('bhqk,bhqkd->bqhd', attn, vg).reshape(B, L, C)
            return o @ w_co + b_co

        def _swiglu(h, w_m1, b_m1, w_m2, b_m2):
            u = h @ w_m1 + b_m1
            a, b = (u[..., :HID], u[..., HID:])
            return jax.nn.silu(a) * b @ w_m2 + b_m2
        key = jax.random.key(seed)
        ks = jax.random.split(key, 24)
        s = 0.02
        inp = {'x': jax.random.normal(ks[0], (2, 1024, C), jnp.float32), 'mod': jax.random.normal(ks[1], (2, C), jnp.float32), 'context': jax.random.normal(ks[2], (2, 256, C), jnp.float32), 'w_ada': jax.random.normal(ks[3], (C, 9 * C), jnp.float32) * s, 'b_ada': jnp.zeros((9 * C,), jnp.float32), 'w_qkv': jax.random.normal(ks[4], (C, 3 * C), jnp.float32) * s, 'b_qkv': jnp.zeros((3 * C,), jnp.float32), 'w_so': jax.random.normal(ks[5], (C, C), jnp.float32) * s, 'b_so': jnp.zeros((C,), jnp.float32), 'w_q': jax.random.normal(ks[6], (C, C), jnp.float32) * s, 'b_q': jnp.zeros((C,), jnp.float32), 'w_kv': jax.random.normal(ks[7], (C, 2 * C), jnp.float32) * s, 'b_kv': jnp.zeros((2 * C,), jnp.float32), 'w_co': jax.random.normal(ks[8], (C, C), jnp.float32) * s, 'b_co': jnp.zeros((C,), jnp.float32), 'w_m1': jax.random.normal(ks[9], (C, 2 * HID), jnp.float32) * s, 'b_m1': jnp.zeros((2 * HID,), jnp.float32), 'w_m2': jax.random.normal(ks[10], (HID, C), jnp.float32) * s, 'b_m2': jnp.zeros((C,), jnp.float32)}
        return inp
    _L0_xcond_all = _L0_xcond_setup()
    _L0_xcond_in = {k: v for k, v in _L0_xcond_all.items() if k in ('w_ada', 'b_ada', 'w_qkv', 'b_qkv', 'w_so', 'b_so', 'w_q', 'b_q', 'w_kv', 'b_kv', 'w_co', 'b_co', 'w_m1', 'b_m1', 'w_m2', 'b_m2')}
    del _L0_xcond_all

    def _L1_xcond_setup():
        import jax, jax.numpy as jnp
        import numpy as np
        EPS = 1e-05

        def _ada_ln(x, c, W_ss, b_ss):
            mu = jnp.mean(x, axis=-1, keepdims=True)
            var = jnp.mean((x - mu) ** 2, axis=-1, keepdims=True)
            h = (x - mu) / jnp.sqrt(var + EPS)
            ss = jax.nn.silu(c) @ W_ss + b_ss
            scale, bias = jnp.split(ss, 2, axis=-1)
            return (1.0 + scale)[:, None, :] * h + bias[:, None, :]
        key = jax.random.key(seed)
        ks = jax.random.split(key, 12)
        B, Lq, Lkv, H = (8, 512, 128, 256)
        s = 0.02
        return {'x_q': jax.random.normal(ks[0], (B, Lq, H), jnp.float32), 'x_kv': jax.random.normal(ks[1], (B, Lkv, H), jnp.float32), 't_vec': jax.random.normal(ks[2], (B, H), jnp.float32), 'Wq': jax.random.normal(ks[3], (H, H), jnp.float32) * s, 'bq': jnp.zeros((H,), jnp.float32), 'Wkv': jax.random.normal(ks[4], (H, 2 * H), jnp.float32) * s, 'bkv': jnp.zeros((2 * H,), jnp.float32), 'Wp': jax.random.normal(ks[5], (H, H), jnp.float32) * s, 'bp': jnp.zeros((H,), jnp.float32), 'Wss_q': jax.random.normal(ks[6], (H, 2 * H), jnp.float32) * s, 'bss_q': jnp.zeros((2 * H,), jnp.float32), 'Wss_kv': jax.random.normal(ks[7], (H, 2 * H), jnp.float32) * s, 'bss_kv': jnp.zeros((2 * H,), jnp.float32)}
    _L1_xcond_all = _L1_xcond_setup()
    _L1_xcond_in = {k: v for k, v in _L1_xcond_all.items() if k in ('Wq', 'bq', 'Wkv', 'bkv', 'Wp', 'bp', 'Wss_q', 'bss_q', 'Wss_kv', 'bss_kv')}
    del _L1_xcond_all
    return {'x': x, 'cond_1024': cond_1024, 'ctx_1024': ctx_1024, 'L0_xcond_w_ada': _L0_xcond_in['w_ada'], 'L0_xcond_b_ada': _L0_xcond_in['b_ada'], 'L0_xcond_w_qkv': _L0_xcond_in['w_qkv'], 'L0_xcond_b_qkv': _L0_xcond_in['b_qkv'], 'L0_xcond_w_so': _L0_xcond_in['w_so'], 'L0_xcond_b_so': _L0_xcond_in['b_so'], 'L0_xcond_w_q': _L0_xcond_in['w_q'], 'L0_xcond_b_q': _L0_xcond_in['b_q'], 'L0_xcond_w_kv': _L0_xcond_in['w_kv'], 'L0_xcond_b_kv': _L0_xcond_in['b_kv'], 'L0_xcond_w_co': _L0_xcond_in['w_co'], 'L0_xcond_b_co': _L0_xcond_in['b_co'], 'L0_xcond_w_m1': _L0_xcond_in['w_m1'], 'L0_xcond_b_m1': _L0_xcond_in['b_m1'], 'L0_xcond_w_m2': _L0_xcond_in['w_m2'], 'L0_xcond_b_m2': _L0_xcond_in['b_m2'], 'L1_xcond_Wq': _L1_xcond_in['Wq'], 'L1_xcond_bq': _L1_xcond_in['bq'], 'L1_xcond_Wkv': _L1_xcond_in['Wkv'], 'L1_xcond_bkv': _L1_xcond_in['bkv'], 'L1_xcond_Wp': _L1_xcond_in['Wp'], 'L1_xcond_bp': _L1_xcond_in['bp'], 'L1_xcond_Wss_q': _L1_xcond_in['Wss_q'], 'L1_xcond_bss_q': _L1_xcond_in['bss_q'], 'L1_xcond_Wss_kv': _L1_xcond_in['Wss_kv'], 'L1_xcond_bss_kv': _L1_xcond_in['bss_kv']}

def reference(x, cond_1024, ctx_1024, L0_xcond_w_ada, L0_xcond_b_ada, L0_xcond_w_qkv, L0_xcond_b_qkv, L0_xcond_w_so, L0_xcond_b_so, L0_xcond_w_q, L0_xcond_b_q, L0_xcond_w_kv, L0_xcond_b_kv, L0_xcond_w_co, L0_xcond_b_co, L0_xcond_w_m1, L0_xcond_b_m1, L0_xcond_w_m2, L0_xcond_b_m2, L1_xcond_Wq, L1_xcond_bq, L1_xcond_Wkv, L1_xcond_bkv, L1_xcond_Wp, L1_xcond_bp, L1_xcond_Wss_q, L1_xcond_bss_q, L1_xcond_Wss_kv, L1_xcond_bss_kv):
    import jax
    import jax.numpy as jnp

    def _L0_xcond_ref(x, mod, context, w_ada, b_ada, w_qkv, b_qkv, w_so, b_so, w_q, b_q, w_kv, b_kv, w_co, b_co, w_m1, b_m1, w_m2, b_m2):
        import jax, jax.numpy as jnp
        import numpy as np
        C = 256
        H = 16
        D = C // H
        WIN = 128
        SHIFT = 64
        TOPK = 16
        HID = 1024
        EPS = 1e-06

        def _ln(x):
            x32 = x.astype(jnp.float32)
            m = x32.mean(-1, keepdims=True)
            v = jnp.mean((x32 - m) ** 2, axis=-1, keepdims=True)
            return ((x32 - m) * jax.lax.rsqrt(v + EPS)).astype(x.dtype)

        def _self_attn(h, w_qkv, b_qkv, w_so, b_so):
            B, L, _ = h.shape
            qkv = h @ w_qkv + b_qkv
            qkv = jnp.roll(qkv, -SHIFT, axis=1)
            nw = L // WIN
            qkv = qkv.reshape(B, nw, WIN, 3, H, D)
            q, k, v = (qkv[:, :, :, 0], qkv[:, :, :, 1], qkv[:, :, :, 2])
            scores = jnp.einsum('bnqhd,bnkhd->bnhqk', q, k) / jnp.sqrt(jnp.float32(D)).astype(h.dtype)
            attn = jax.nn.softmax(scores, axis=-1)
            o = jnp.einsum('bnhqk,bnkhd->bnqhd', attn, v).reshape(B, L, C)
            o = jnp.roll(o, SHIFT, axis=1)
            return o @ w_so + b_so

        def _topk_cross_attn(h, ctx, w_q, b_q, w_kv, b_kv, w_co, b_co):
            B, L, _ = h.shape
            Lc = ctx.shape[1]
            q = (h @ w_q + b_q).reshape(B, L, H, D)
            kv = (ctx @ w_kv + b_kv).reshape(B, Lc, 2, H, D)
            k, v = (kv[:, :, 0], kv[:, :, 1])
            scores = jnp.einsum('bqhd,bkhd->bhqk', q, k) / jnp.sqrt(jnp.float32(D)).astype(h.dtype)
            top_s, top_i = jax.lax.top_k(scores, TOPK)
            attn = jax.nn.softmax(top_s, axis=-1)
            v_bh = jnp.transpose(v, (0, 2, 1, 3))
            vg = jnp.take_along_axis(v_bh[:, :, None, :, :], top_i[..., None], axis=3)
            o = jnp.einsum('bhqk,bhqkd->bqhd', attn, vg).reshape(B, L, C)
            return o @ w_co + b_co

        def _swiglu(h, w_m1, b_m1, w_m2, b_m2):
            u = h @ w_m1 + b_m1
            a, b = (u[..., :HID], u[..., HID:])
            return jax.nn.silu(a) * b @ w_m2 + b_m2
        m = jax.nn.silu(mod) @ w_ada + b_ada
        sh_msa, sc_msa, g_msa, sh_mca, sc_mca, g_mca, sh_mlp, sc_mlp, g_mlp = [m[:, i * C:(i + 1) * C][:, None, :] for i in range(9)]
        h = _ln(x) * (1 + sc_msa) + sh_msa
        h = _self_attn(h, w_qkv, b_qkv, w_so, b_so)
        x = x + h * g_msa
        h = _ln(x) * (1 + sc_mca) + sh_mca
        h = _topk_cross_attn(h, context, w_q, b_q, w_kv, b_kv, w_co, b_co)
        x = x + h * g_mca
        h = _ln(x) * (1 + sc_mlp) + sh_mlp
        h = _swiglu(h, w_m1, b_m1, w_m2, b_m2)
        x = x + h * g_mlp
        return x

    def _L1_xcond_ref(x_q, x_kv, t_vec, Wq, bq, Wkv, bkv, Wp, bp, Wss_q, bss_q, Wss_kv, bss_kv):
        import jax, jax.numpy as jnp
        import numpy as np
        EPS = 1e-05

        def _ada_ln(x, c, W_ss, b_ss):
            mu = jnp.mean(x, axis=-1, keepdims=True)
            var = jnp.mean((x - mu) ** 2, axis=-1, keepdims=True)
            h = (x - mu) / jnp.sqrt(var + EPS)
            ss = jax.nn.silu(c) @ W_ss + b_ss
            scale, bias = jnp.split(ss, 2, axis=-1)
            return (1.0 + scale)[:, None, :] * h + bias[:, None, :]
        B, Lq, H = x_q.shape
        Lkv = x_kv.shape[1]
        nh = 16
        dh = H // nh
        xq = _ada_ln(x_q, t_vec, Wss_q, bss_q)
        xkv = _ada_ln(x_kv, t_vec, Wss_kv, bss_kv)
        q = (xq @ Wq + bq).reshape(B, Lq, nh, dh)
        kv = (xkv @ Wkv + bkv).reshape(B, Lkv, 2, nh, dh)
        k = kv[:, :, 0]
        v = kv[:, :, 1]
        scores = jnp.einsum('bqhd,bkhd->bhqk', q, k) / jnp.sqrt(jnp.float32(dh))
        attn = jax.nn.softmax(scores, axis=-1)
        out = jnp.einsum('bhqk,bkhd->bqhd', attn, v).reshape(B, Lq, H)
        return x_q + (out @ Wp + bp)
    x = _L0_xcond_ref(x, cond_1024, ctx_1024, L0_xcond_w_ada, L0_xcond_b_ada, L0_xcond_w_qkv, L0_xcond_b_qkv, L0_xcond_w_so, L0_xcond_b_so, L0_xcond_w_q, L0_xcond_b_q, L0_xcond_w_kv, L0_xcond_b_kv, L0_xcond_w_co, L0_xcond_b_co, L0_xcond_w_m1, L0_xcond_b_m1, L0_xcond_w_m2, L0_xcond_b_m2)
    x = _L1_xcond_ref(x, ctx_1024, cond_1024, L1_xcond_Wq, L1_xcond_bq, L1_xcond_Wkv, L1_xcond_bkv, L1_xcond_Wp, L1_xcond_bp, L1_xcond_Wss_q, L1_xcond_bss_q, L1_xcond_Wss_kv, L1_xcond_bss_kv)
    return x

_drawn_inputs = setup_inputs


def setup_inputs(seed=0):
    import zlib

    import numpy as np

    out = dict(_drawn_inputs(seed))
    spreads = {'L0_xcond_b_ada': (0.0, 0.389),
     'L0_xcond_b_qkv': (0.0, 0.8),
     'L0_xcond_b_so': (0.0, 0.37),
     'L0_xcond_b_q': (0.0, 0.8),
     'L0_xcond_b_kv': (0.0, 0.8),
     'L0_xcond_b_co': (0.0, 0.409),
     'L0_xcond_b_m1': (0.0, 0.8),
     'L0_xcond_b_m2': (0.0, 1.388),
     'L1_xcond_bq': (0.0, 2.0),
     'L1_xcond_bkv': (0.0, 0.8),
     'L1_xcond_bp': (0.0, 0.631),
     'L1_xcond_bss_q': (0.0, 2.0),
     'L1_xcond_bss_kv': (0.0, 2.0)}
    factors = {'L0_xcond_w_qkv': 8.0,
     'L0_xcond_w_so': 6.081,
     'L0_xcond_w_q': 5.125,
     'L0_xcond_w_kv': 3.439,
     'L0_xcond_w_co': 3.212,
     'L0_xcond_w_m1': 6.137,
     'L0_xcond_w_m2': 6.121,
     'L1_xcond_Wq': 57.86,
     'L1_xcond_Wss_q': 64.0,
     'L1_xcond_Wkv': 3.855,
     'L1_xcond_Wp': 3.72,
     'L1_xcond_Wss_kv': 8.0}
    for name, (base, spread) in spreads.items():
        noise = np.random.default_rng([zlib.crc32(name.encode()), seed]).standard_normal(out[name].shape)
        drawn = base * np.exp(spread * noise) if base else spread * noise
        out[name] = jnp.asarray(drawn.astype(out[name].dtype))
    for name, factor in factors.items():
        out[name] = (out[name] * factor).astype(out[name].dtype)
    return out
```

```python
from contextlib import ExitStack

import concourse.bass as bass
import concourse.mybir as mybir

F32 = mybir.dt.float32
F16 = mybir.dt.float16
BF16 = mybir.dt.bfloat16
ALU = mybir.AluOpType
ACT = mybir.ActivationFunctionType
AX = mybir.AxisListType

P = 128
SLOT = 32
FAR = 2.0 ** 100


class Program:

    def __init__(self, nc, ctx):
        self.nc, self.ctx = nc, ctx
        self.queue = {"sp": [], "pe": [], "act": [], "dve": [], "pool": []}
        self.waited = {e: {} for e in self.queue}
        self.count, self.sems, self.marks = {}, {}, {}

    def sem(self, name):
        if name not in self.sems:
            self.sems[name] = self.ctx.enter_context(self.nc.semaphore(name))
            self.count[name] = 0
        return self.sems[name]

    def op(self, engine, emit, signal=None, by=1):
        if signal is None:
            self.queue[engine].append(emit)
            return None
        s = self.sem(signal)
        self.count[signal] += by
        self.queue[engine].append(lambda e: emit(e).then_inc(s, by))
        return (signal, self.count[signal])

    def wait(self, engine, *marks):
        for mark in marks:
            name, value = mark
            if self.waited[engine].get(name, 0) >= value:
                continue
            self.waited[engine][name] = value
            s = self.sems[name]
            self.queue[engine].append(lambda e, s=s, v=value: e.wait_ge(s, v))


class Ring:

    def __init__(self, tiles):
        self.tiles, self.free = tiles, [[] for _ in tiles]
        self.idle = list(range(len(tiles)))

    def ready(self):
        return bool(self.idle)

    def take(self):
        i = self.idle.pop(0)
        return i, self.tiles[i], self.free[i]

    def release(self, i, *marks):
        self.idle.append(i)
        self.free[i] = list(marks)


def build(nc, A, out):
    B, L, C = A["x"].shape
    H = 16
    D = C // H
    TOP = 16
    SHIFT = 64
    HID = A["L0_xcond_w_m2"].shape[0]
    CC = C // P
    LT = L // P
    HC = HID // P
    G4 = P // SLOT
    NG = H // G4
    assert (CC, LT, NG, D) == (2, 2, 4, 16) and TOP == 16 and SHIFT * 2 == P
    QSCALE = float(D) ** -0.5

    with ExitStack() as ctx:
        prog = Program(nc, ctx)
        op, wait = prog.op, prog.wait

        def sb(name, shape, dt):
            return ctx.enter_context(nc.sbuf_tensor(name, shape, dt))

        def ring(name, n, shape, dt):
            return Ring([sb(f"{name}{i}", shape, dt) for i in range(n)])

        def psum(name, n):
            return Ring([ctx.enter_context(nc.psum_tensor(f"{name}{i}", [P, 512], F32)) for i in range(n)])

        bank_score = psum("bank_score", 2)
        bank_prob = psum("bank_prob", 2)
        bank_out = psum("bank_out", 1)
        bank_any = psum("bank_any", 3)

        ident32 = sb("ident32", [P, P], F32)
        ident16 = sb("ident16", [P, P], BF16)
        ones_row = sb("ones_row", [1, P], F16)
        minus_half = sb("minus_half", [P, LT], F32)

        NB = {"ada": 18, "qkv": 6, "so": 2, "q": 2, "kv": 4, "co": 2, "m1": 16, "m2": 2,
              "bq": 2, "bkv": 4, "bp": 2, "ssq": 4, "sskv": 4}
        bias_src = {"ada": "L0_xcond_b_ada", "qkv": "L0_xcond_b_qkv", "so": "L0_xcond_b_so",
                    "q": "L0_xcond_b_q", "kv": "L0_xcond_b_kv", "co": "L0_xcond_b_co",
                    "m1": "L0_xcond_b_m1", "m2": "L0_xcond_b_m2", "bq": "L1_xcond_bq",
                    "bkv": "L1_xcond_bkv", "bp": "L1_xcond_bp", "ssq": "L1_xcond_bss_q",
                    "sskv": "L1_xcond_bss_kv"}
        bias_at, rows = {}, 0
        for name, n in NB.items():
            bias_at[name] = rows
            rows += n
        NBR = rows
        bias_rows = sb("bias_rows", [NBR, P], F32)
        bias_col = sb("bias_col", [P, NBR], F32)
        q_bias = sb("q_bias", [P, 3 * CC], F32)
        half_bias = sb("half_bias", [P, HC], F32)

        W = {}
        for name, src, k, n, scale in (
            ("qkv", "L0_xcond_w_qkv", CC, 3 * C, 1.0), ("so", "L0_xcond_w_so", CC, C, 1.0),
            ("q", "L0_xcond_w_q", CC, C, QSCALE), ("kv", "L0_xcond_w_kv", CC, 2 * C, 1.0),
            ("co", "L0_xcond_w_co", CC, C, 1.0), ("m1", "L0_xcond_w_m1", CC, 2 * HID, 1.0),
            ("m2", "L0_xcond_w_m2", HC, C, 1.0), ("Wq", "L1_xcond_Wq", CC, C, QSCALE),
            ("Wkv", "L1_xcond_Wkv", CC, 2 * C, 1.0), ("Wp", "L1_xcond_Wp", CC, C, 1.0),
        ):
            W[name] = dict(src=A[src].rearrange("(k p) n -> p k n", p=P), k=k, n=n, scale=scale,
                           hi=sb(f"w_{name}_hi", [P, k, n], F16), lo=sb(f"w_{name}_lo", [P, k, n], F16))
        value_bias = {}
        for name, src, at in (("self", "L0_xcond_b_qkv", 2 * C), ("top", "L0_xcond_b_kv", C),
                              ("last", "L1_xcond_bkv", C)):
            value_bias[name] = dict(src=A[src][at:at + C].rearrange("(o n) -> o n", o=1),
                                    raw=sb(f"vb_{name}", [1, C], F32), hi=sb(f"vb_{name}_hi", [1, C], F16),
                                    lo=sb(f"vb_{name}_lo", [1, C], F16))

        NA = NB["ada"]
        cond = sb("cond", [B, C], F32)
        cond_T = sb("cond_T", [P, CC, B], F32)
        cond_t = sb("cond_t", [P, CC, B], F32)
        cond_s = sb("cond_s", [P, CC, B], F32)
        ada = sb("ada", [P, NA, B], F32)
        gate_bias = sb("gate_bias", [P, 3 * CC, B], F32)
        half_gate = sb("half_gate", [P, CC, B], F32)
        ssq = sb("ssq", [P, NB["ssq"], B], F32)
        sskv = sb("sskv", [P, NB["sskv"], B], F32)

        X_ring = ring("x_tile", 4, [P, LT, C], F32)
        ctx_ring = ring("ctx_tile", 2, [P, LT, C], F32)
        stats_ring = ring("stats", 4, [P, LT, 6], F32)
        mv_ring = ring("mean_var", 4, [P, LT, 2], F32)
        rstd_ring = ring("rstd", 4, [P, 3, LT], F32)
        norm_ring = ring("normed", 2, [P, LT, C], F32)
        full_ring = ring("full", 3, [P, CC, L], F32)
        pair_ring = ring("pair", 5, [P, 2, CC, L], F16)
        tanh_ring = ring("tanh", 2, [P, 2, L], F32)
        gated_ring = ring("gated", 2, [P, 2, L], F32)
        hid_ring = ring("hid", 1, [P, 2, HC, L], F16)
        prob_ring = ring("prob", 3, [P, 512], F32)
        osum_ring = ring("osum", 3, [P, NG, L], F32)
        recip_ring = ring("recip", 4, [P, H], F32)
        rest_ring = ring("rest", 4, [P, L], F32)
        best_ring = ring("best", 4, [P, LT, 8], F32)
        far_ring = ring("far", 10, [P, LT, L], BF16)
        rowmax_ring = ring("rowmax", 3, [P, 8, LT, 8], F32)
        guard_ring = ring("guard", 3, [16, P], F16)

        NR = 3 * D
        PARTS = {"q": (0, 1, 0), "k": (0, 0, 1)}
        stacks, slots = {}, []
        for pair_of in (("top0", "top1"), ("self0", "last0")):
            halves = {w: sb(f"{w}_stack_{pair_of[0]}_{pair_of[1]}", [P, H, L], F16) for w in "qk"}
            for name, base in zip(pair_of, (0, P // 2)):
                slots.append(dict(
                    name=name, tile=halves, base=base,
                    q=halves["q"][base:base + NR + 1, :, :], k=halves["k"][base:base + NR + 1, :, :],
                    v=sb(f"v_{name}", [P, LT, H, SLOT], F32),
                    dq=nc.dram_tensor(f"dq_{name}", (2, C, L), F16, kind="Internal").ap(),
                    dk=nc.dram_tensor(f"dk_{name}", (2, C, L), F16, kind="Internal").ap(),
                    dm=nc.dram_tensor(f"dm_{name}", (H, LT, P), F16, kind="Internal").ap()))
        for kind in ("top", "self", "last"):
            stacks[kind] = Ring([s for s in slots if s["name"][:-1] == kind])
        stage_cols = 2048
        stage = [sb(f"stage{i}", [P, stage_cols // 2], F32) for i in range(2)]

        def mm(o, lhsT, rhs, start, stop, signal=None):
            return op("pe", lambda e: e.matmul(o, lhsT, rhs, start=start, stop=stop), signal)

        def turn(o, i, signal=None):
            n = i.partition_size()
            return op("pe", lambda e: e.transpose(o, i, ident32[0:n, 0:n]), signal)

        def act(o, i, f, signal=None, **kw):
            return op("act", lambda e: e.activation(o, i, f, **kw), signal)

        def dma(o, i, signal):
            return op("sp", lambda e: e.dma_start(o, i), signal, 16)

        def dve_tt(o, a, b, f, signal=None):
            return op("dve", lambda e: e.tensor_tensor(o, a, b, f), signal)

        def dve_ts(o, a, s1, s2, f0, f1, signal=None):
            return op("dve", lambda e: e.tensor_scalar(o, a, s1, s2, f0, f1), signal)

        def dve_stt(o, a, s, b, f0, f1, signal=None):
            return op("dve", lambda e: e.scalar_tensor_tensor(o, a, s, b, f0, f1), signal)

        def pool_tt(o, a, b, f, signal=None):
            return op("pool", lambda e: e.tensor_tensor(o, a, b, f), signal)

        def pool_ts(o, a, s1, s2, f0, f1, signal=None):
            return op("pool", lambda e: e.tensor_scalar(o, a, s1, s2, f0, f1), signal)

        def dve_max8(o, i, signal):
            return op("dve", lambda e: e.max(o, i), signal)

        def dve_replace(o, what, i, signal):
            return op("dve", lambda e: e.match_replace(o, what, i, -FAR), signal)

        def prologue():
            marks = prog.marks
            z = op("pool", lambda e: e.memset(ident32[:, :], 0.0), "const")
            z = op("pool", lambda e: e.memset(ident16[:, :], 0.0), "const")
            wait("pool", z)
            for t in (ident32, ident16):
                one = op("pool", lambda e, t=t: e.affine_select(
                    out=t[:, :], in_=t[:, :], compare_op=ALU.not_equal, fill=1.0, base=0,
                    pattern=[[-1, P]], channel_multiplier=1), "const")
            marks["const"] = one
            op("dve", lambda e: e.memset(ones_row[:, :], 1.0), "const_dve")
            op("dve", lambda e: e.memset(minus_half[:, :], -0.5), "const_dve")
            for kind in stacks:
                for s in stacks[kind].tiles:
                    lo = s["base"] + SLOT
                    op("dve", lambda e, s=s, lo=lo: e.memset(s["tile"]["k"][lo:lo + SLOT, :, :], 1.0), "const_dve")
                    marks["const2"] = op("dve", lambda e, s=s: e.memset(s["v"][:, :, :, D:SLOT], 1.0),
                                         "const_dve")
            for name, src in bias_src.items():
                at = bias_at[name]
                m = dma(bias_rows[at:at + NB[name], :], A[src].rearrange("(m p) -> m p", p=P), "small_in")
            for v in value_bias.values():
                m = dma(v["raw"][:, :], v["src"], "small_in")
            m = dma(cond[:, :], A["cond_1024"], "small_in")
            wait("pe", marks["const"], m)
            i, bank, _ = bank_any.take()
            turn(bank[:, 0:NBR], bias_rows[:, :])
            for c in range(CC):
                t = turn(bank[:, 128 + B * c:128 + B * (c + 1)], cond[:, c * P:(c + 1) * P], "pe_pre")
            wait("act", t)
            act(bias_col[:, :], bank[:, 0:NBR], ACT.Copy)
            cT = bank[:, 128:128 + CC * B].rearrange("p (c b) -> p c b", c=CC)
            act(cond_T[:, :, :], cT, ACT.Copy)
            t = act(cond_t[:, :, :], cT, ACT.Tanh, "act_pre", scale=0.5)
            bank_any.release(i, t)
            wait("dve", t, m)
            t = dve_stt(cond_s[:, :, :], cond_t[:, :, :], 1.0, cond_T[:, :, :], ALU.add, ALU.mult, "dve_pre")
            wait("dve", t)
            t = dve_ts(cond_T[:, :, :], cond_s[:, :, :], 0.5, None, ALU.mult, ALU.bypass, "dve_pre")
            marks["cond"] = t
            for j, name in enumerate(("qkv", "q", "bq")):
                dve_ts(q_bias[:, CC * j:CC * (j + 1)], bias_col[:, bias_at[name]:bias_at[name] + CC],
                       QSCALE, None, ALU.mult, ALU.bypass)
            marks["bias"] = dve_ts(half_bias[:, :], bias_col[:, bias_at["m1"]:bias_at["m1"] + HC], 0.5, None,
                                   ALU.mult, ALU.bypass, "dve_pre")
            for v in value_bias.values():
                op("dve", lambda e, v=v: e.tensor_copy(v["hi"][:, :], v["raw"][:, :]), "dve_pre")
            wait("dve", ("dve_pre", prog.count["dve_pre"]))
            for v in value_bias.values():
                marks["vbias"] = dve_tt(v["lo"][:, :], v["raw"][:, :], v["hi"][:, :], ALU.subtract, "dve_pre")
            yield
            stage_free = [[], []]
            turn_no = [0]

            def staged(src, k, n):
                i = turn_no[0] % 2
                turn_no[0] += 1
                wait("sp", *stage_free[i])
                view = stage[i][:, 0:k * n].rearrange("p (k n) -> p k n", k=k)
                return i, view, dma(view, src, f"stage_in{i}")

            for dst, src, bias, total in ((ada, "L0_xcond_w_ada", "ada", NA), (ssq, "L1_xcond_Wss_q", "ssq", 4),
                                          (sskv, "L1_xcond_Wss_kv", "sskv", 4)):
                for m0 in range(0, total, 4):
                    n = min(4, total - m0)
                    si, view, landed = staged(
                        A[src].rearrange("(k p) n -> p k n", p=P)[:, :, m0 * P:(m0 + n) * P], CC, n * P)
                    i, bank, free = bank_any.take()
                    wait("pe", landed, marks["cond"], *free)
                    for m in range(n):
                        for c in range(CC):
                            t = mm(bank[:, m * B:(m + 1) * B], view[:, c, m * P:(m + 1) * P], cond_T[:, c, :],
                                   c == 0, c == CC - 1, "pe_pre" if (m, c) == (n - 1, CC - 1) else None)
                    stage_free[si] = [t]
                    at = bias_at[bias] + m0
                    wait("dve", t)
                    t = dve_tt(dst[:, m0:m0 + n, :], bank[:, 0:n * B].rearrange("p (m b) -> p m b", b=B),
                               bias_col[:, at:at + n].unsqueeze(2).broadcast_to([P, n, B]), ALU.add, "dve_pre")
                    bank_any.release(i, t)
            wait("dve", t)
            for i in (1, 4, 7):
                dve_ts(ada[:, 2 * i:2 * i + 2, :], ada[:, 2 * i:2 * i + 2, :], 1.0, None, ALU.add, ALU.bypass)
            for s in (ssq, sskv):
                dve_ts(s[:, 0:2, :], s[:, 0:2, :], 1.0, None, ALU.add, ALU.bypass)
            dve_ts(half_gate[:, :, :], ada[:, 16:18, :], 0.5, None, ALU.mult, ALU.bypass)
            for j, name in enumerate(("so", "co", "m2")):
                g = 2 * (3 * j + 2)
                at = bias_at[name]
                marks["ada"] = dve_tt(gate_bias[:, CC * j:CC * (j + 1), :], ada[:, g:g + 2, :],
                                      bias_col[:, at:at + 2].unsqueeze(2).broadcast_to([P, CC, B]),
                                      ALU.mult, "dve_pre")
            for name in ("qkv", "so", "q", "kv", "co", "m1", "m2", "Wq", "Wkv", "Wp"):
                w = W[name]
                width = min(w["n"], stage_cols // 2 // w["k"] // P * P)
                for n0 in range(0, w["n"], width):
                    n = min(width, w["n"] - n0)
                    si, view, landed = staged(w["src"][:, :, n0:n0 + n], w["k"], n)
                    hi, lo = w["hi"][:, :, n0:n0 + n], w["lo"][:, :, n0:n0 + n]
                    parts = [(0, n, w["scale"])]
                    if name == "qkv":
                        parts = [(max(0, a - n0), min(n, b - n0), s) for a, b, s in
                                 ((0, C, QSCALE), (C, 3 * C, 1.0)) if max(n0, a) < min(n0 + n, b)]
                    wait("act", landed)
                    for a, b, s in parts:
                        t = act(hi[:, :, a:b], view[:, :, a:b], ACT.Copy, "act_pre", scale=s)
                    wait("dve", t)
                    for a, b, s in parts:
                        t = dve_stt(lo[:, :, a:b], view[:, :, a:b], s, hi[:, :, a:b], ALU.mult, ALU.subtract,
                                    "dve_pre")
                    stage_free[si] = [t]
                W[name]["mark"] = t
                yield

        def held(*rings):
            while not all(r.ready() for r in rings):
                yield

        def split_in(w):
            while "mark" not in w:
                yield

        def layer_norm(src, src_marks, scale, shift, eps, result):
            yield from held(stats_ring, mv_ring, rstd_ring, norm_ring)
            si, stats, sfree = stats_ring.take()
            mi, mv, mfree = mv_ring.take()
            ri, rstd, rfree = rstd_ring.take()
            ni, norm, nfree = norm_ring.take()
            wait("dve", *src_marks, *sfree, *mfree)
            for t in range(LT):
                m = op("dve", lambda e, t=t: e.bn_stats(stats[:, t, :], src[:, t, :]), "dve_ln")
            yield
            wait("dve", m)
            for t in range(LT):
                m = op("dve", lambda e, t=t: e.bn_aggr(mv[:, t, :], stats[:, t, :]), "dve_ln")
            stats_ring.release(si, m)
            yield
            wait("pool", m, prog.marks["const2"], *rfree, *nfree)
            m = pool_ts(rstd[:, 0, :], mv[:, :, 1], eps, 1.0, ALU.add, ALU.mult, "pool_ln")
            wait("pool", m)
            m = pool_tt(rstd[:, 1, :], rstd[:, 0, :], minus_half[:, :], ALU.pow, "pool_ln")
            wait("pool", m)
            m = pool_tt(rstd[:, 0, :], mv[:, :, 0], rstd[:, 1, :], ALU.mult, "pool_ln")
            wait("pool", m)
            m = pool_ts(rstd[:, 2, :], rstd[:, 0, :], -1.0, 0.0, ALU.mult, ALU.add, "pool_ln")
            mv_ring.release(mi, m)
            wait("pool", m)
            for t in range(LT):
                m = pool_ts(norm[:, t, :], src[:, t, :], rstd[:, 1, t:t + 1], rstd[:, 2, t:t + 1],
                            ALU.mult, ALU.add, "pool_ln")
            rstd_ring.release(ri, m)
            result["read"] = m
            yield
            yield
            yield from bank_to_split(result)
            bi, bank, bfree = bank_any.take()
            wait("pe", m, *bfree)
            for c in range(CC):
                for t in range(LT):
                    m = turn(bank[:, c * L + t * P:c * L + (t + 1) * P], norm[:, t, c * P:(c + 1) * P],
                             "pe_turn" if (c, t) == (CC - 1, LT - 1) else None)
            norm_ring.release(ni, m)
            yield from split(bi, bank, m, [(scale(c), shift(c)) for c in range(CC)], result)

        def bank_to_split(result):
            yield from held(bank_any, full_ring, pair_ring)
            result["full"], result["taken"] = full_ring.take(), pair_ring.take()

        def split(bi, bank, mark, affine, result):
            fi, full, ffree = result["full"]
            pi, pair, pfree = result["taken"]
            yield
            wait("act", mark, *ffree, *pfree)
            view = bank[:, :].rearrange("p (c l) -> p c l", c=CC)
            if affine is None:
                act(full[:, :, :], view, ACT.Copy)
                m = act(pair[:, 0, :, :], view, ACT.Copy, "act_split")
            else:
                for c, (s, b) in enumerate(affine):
                    kw = dict(bias=b) if s is None else dict(scale=s, bias=b)
                    act(full[:, c, :], view[:, c, :], ACT.Identity, **kw)
                    m = act(pair[:, 0, c, :], view[:, c, :], ACT.Identity, "act_split", **kw)
            bank_any.release(bi, m)
            yield
            wait("pool", m)
            m2 = pool_tt(pair[:, 1, :, :], full[:, :, :], pair[:, 0, :, :], ALU.subtract, "pool_split")
            full_ring.release(fi, m2)
            result.update(pair=pair, index=pi, marks=[m, m2])
            yield

        def project(bank_at, w, cols, pair, chunks, signal):
            for k in range(chunks):
                for n, (a, b) in enumerate((("hi", 0), ("hi", 1), ("lo", 0))):
                    last = k == chunks - 1 and n == 2
                    m = mm(bank_at, w[a][:, k, cols], pair[:, b, k, :], k == 0 and n == 0, last,
                           signal if last else None)
            return m

        def to_stack(kind_slot, which, pair, pi, marks):
            s, name = kind_slot[which], kind_slot["name"] + which
            d = kind_slot["d" + which]
            wait("sp", prog.marks["const2"], *marks, *kind_slot.get("free_d" + which, []))
            for part in range(2):
                m = dma(d[part].rearrange("(c p) l -> p c l", p=P), pair[:, part, :, :], f"to_{name}")
            kind_slot["written" + which] = m
            pair_ring.release(pi, m)
            wait("sp", m, *kind_slot.get("free", []))
            for r, part in enumerate(PARTS[which]):
                m = dma(s[r * D:(r + 1) * D, :, :], d[part].rearrange("(h d) l -> d h l", d=D), f"from_{name}")
            kind_slot["free_d" + which] = [m]
            return m

        def project_values(w, col0, pair, marks, bias, slot, first_free):
            yield from split_in(w)
            yield from held(bank_any)
            bi, bank, bfree = bank_any.take()
            wait("pe", *marks, w["mark"], prog.marks["const2"], *bfree)
            for t in range(LT):
                o = bank[:, t * C:(t + 1) * C]
                mm(o, ones_row[:, :], bias["hi"][:, :], True, False)
                mm(o, ones_row[:, :], bias["lo"][:, :], False, False)
                for k in range(CC):
                    for n, (a, b) in enumerate(((0, "hi"), (1, "hi"), (0, "lo"))):
                        last = k == CC - 1 and n == 2
                        m = mm(o, pair[:, a, k, t * P:(t + 1) * P], w[b][:, k, col0:col0 + C], False, last,
                               "pe_v" if last and t == LT - 1 else None)
            yield
            wait("act", m, *first_free)
            v = act(slot["v"][:, :, :, 0:D].rearrange("p t h d -> p (t h) d"),
                    bank[:, :].rearrange("p (g d) -> p g d", d=D), ACT.Copy, "act_v")
            bank_any.release(bi, v)
            slot["v_mark"] = v
            slot["v_read"] = m

        def project_stack(w, col0, bias_col0, is_q, qj, pair, marks, slot, which):
            yield from split_in(w)
            res = {}
            yield from bank_to_split(res)
            bi, bank, bfree = bank_any.take()
            wait("pe", *marks, w["mark"], *bfree)
            for c in range(CC):
                m = project(bank[:, c * L:(c + 1) * L], w, slice(col0 + c * P, col0 + (c + 1) * P), pair, CC,
                            "pe_qk")
            slot["pair_read"] = m
            if is_q:
                aff = [(None, q_bias[:, CC * qj + c:CC * qj + c + 1]) for c in range(CC)]
            else:
                aff = [(None, bias_col[:, bias_col0 + c:bias_col0 + c + 1]) for c in range(CC)]
            yield from split(bi, bank, m, aff, res)
            slot[which + "_mark"] = to_stack(slot, which, res["pair"], res["index"], res["marks"])
            yield

        def guard(slot, rm, h0, n, mark, done):
            yield from held(bank_any, guard_ring)
            bi, bank, bfree = bank_any.take()
            gi, g, gfree = guard_ring.take()
            wait("pe", mark, *bfree)
            m = turn(bank[0:n * LT, 0:P], rm[:, 0:n, :, 0].rearrange("p h t -> p (h t)"), "pe_turn")
            yield
            wait("act", m, *gfree)
            m = act(g[0:n * LT, :], bank[0:n * LT, 0:P], ACT.Copy, "act_guard", scale=-1.0)
            bank_any.release(bi, m)
            name = slot["name"]
            wait("sp", m, *slot.get("free_dm", []))
            m = dma(slot["dm"][h0:h0 + n].rearrange("h t l -> (h t) l"), g[0:n * LT, :], f"to_m{name}")
            guard_ring.release(gi, m)
            wait("sp", m, *slot.get("free", []))
            m = dma(slot["q"][NR:NR + 1, h0:h0 + n, :],
                    slot["dm"][h0:h0 + n].rearrange("(o h) t l -> o h (t l)", o=1), f"from_m{name}")
            slot["free_dm"] = [m]
            done["mark"] = m
            yield

        def attend_group(slot, osum, g, window, far, marks):
            oi, obank, ofree = bank_out.take()
            q, k, v = slot["q"], slot["k"], slot["v"]
            wait("pe", slot["v_mark"], slot["q_mark"], slot["k_mark"], prog.marks["const2"], *marks)
            step = 2 if window else 1
            todo = []
            for h0 in range(g * G4, (g + 1) * G4, step):
                bi, bank, bfree = bank_prob.take()
                pi, prob, pfree = prob_ring.take()
                wait("pe", *bfree)
                for h in range(h0, h0 + step):
                    for t in range(LT):
                        if window:
                            at = ((h - h0) * LT + t) * P
                            m = mm(bank[:, at:at + P], k[:, h, t * P:(t + 1) * P], q[:, h, t * P:(t + 1) * P],
                                   True, True, "pe_prob")
                            continue
                        o = bank[:, t * L:(t + 1) * L]
                        m = mm(o, k[:, h, t * P:(t + 1) * P], q[:, h, :], True, far is None,
                               "pe_prob" if far is None else None)
                        if far is not None:
                            fi, ftile, fmark = far[h % G4]
                            wait("pe", fmark)
                            for j in range(LT):
                                m = mm(o[:, j * P:(j + 1) * P], ftile[:, j, t * P:(t + 1) * P], ident16[:, :],
                                       False, j == LT - 1, "pe_prob" if j == LT - 1 else None)
                if far is not None:
                    far_ring.release(far[h0 % G4][0], m)
                wait("act", m, *pfree)
                e = act(prob[:, :], bank[:, :], ACT.Exp, "act_exp")
                bank_prob.release(bi, e)
                todo.append((h0, pi, prob, e))
                if len(todo) == 2:
                    values_of(*todo.pop(0), window, step, g, obank, v, ofree)
            while todo:
                m = values_of(*todo.pop(0), window, step, g, obank, v, ofree)
            wait("act", m, *osum["free"])
            osum["mark"] = act(osum["tile"][:, g, :], obank[:, 0:L], ACT.Copy, "act_osum")
            bank_out.release(oi, osum["mark"])
            return m

        def values_of(h0, pi, prob, e, window, step, g, obank, v, ofree):
            wait("pe", e, *ofree)
            for h in range(h0, h0 + step):
                j = (h - g * G4) * SLOT
                for t in range(LT):
                    if window:
                        m = mm(obank[j:j + SLOT, t * P:(t + 1) * P], v[:, t, h, :],
                               prob[:, ((h - h0) * LT + t) * P:((h - h0) * LT + t + 1) * P], True, True, "pe_pv")
                    else:
                        m = mm(obank[j:j + SLOT, 0:L], v[:, t, h, :], prob[:, t * L:(t + 1) * L],
                               t == 0, t == LT - 1, "pe_pv")
            prob_ring.release(pi, m)
            return m

        def attend(slot, window, osum):
            q, k = slot["q"], slot["k"]
            done = []
            for h8 in range(0, H, 8):
                yield from held(rowmax_ring)
                ri, rm, rfree = rowmax_ring.take()
                step = 2 if window else 1
                for h0 in range(h8, h8 + 8, step):
                    yield from held(bank_any)
                    bi, bank, bfree = bank_any.take()
                    wait("pe", slot["q_mark"], slot["k_mark"], *bfree)
                    for h in range(h0, h0 + step):
                        for t in range(LT):
                            if window:
                                at = ((h - h0) * LT + t) * P
                                m = mm(bank[:, at:at + P], q[0:NR, h, t * P:(t + 1) * P],
                                       k[0:NR, h, t * P:(t + 1) * P], True, True, "pe_score")
                            else:
                                m = mm(bank[:, t * L:(t + 1) * L], q[0:NR, h, t * P:(t + 1) * P], k[0:NR, h, :],
                                       True, True, "pe_score")
                    yield
                    wait("dve", m, *rfree)
                    n = 2 * step
                    m = op("dve", lambda e, rm=rm, bank=bank, h0=h0, h8=h8, step=step, n=n: e.tensor_reduce(
                        rm[:, h0 - h8:h0 - h8 + step, :, 0], bank[:, :].rearrange(
                            "p (h t k) -> p h t k", h=step, t=LT), AX.X, ALU.max), "dve_max")
                    bank_any.release(bi, m)
                d = {}
                yield
                yield from guard(slot, rm, h8, 8, m, d)
                rowmax_ring.release(ri, d["mark"])
                done.append(d["mark"])
            for _ in range(4):
                yield
            for g in range(NG):
                while not (bank_out.ready() and bank_prob.ready() and prob_ring.ready()):
                    yield
                m = attend_group(slot, osum, g, window, None, [done[g // 2]])
                yield
            slot["free"] = [m]

        def finish_attention(osum, w, scale, shift, X, result):
            yield from split_in(w)
            yield from held(norm_ring)
            ni, norm, nfree = norm_ring.take()
            for t in range(LT):
                yield from held(bank_any, recip_ring)
                bi, bank, bfree = bank_any.take()
                ri, rc, rfree = recip_ring.take()
                wait("pe", osum["mark"], *bfree)
                for g in range(NG):
                    m = turn(bank[:, g * P:(g + 1) * P], osum["tile"][:, g, t * P:(t + 1) * P],
                             "pe_turn" if g == NG - 1 else None)
                yield
                heads = bank[:, :].rearrange("p (h s) -> p h s", s=SLOT)
                wait("dve", m, *rfree, *nfree)
                m2 = op("dve", lambda e, rc=rc, heads=heads: e.reciprocal(rc[:, :], heads[:, :, D]), "dve_norm")
                yield
                wait("dve", m2)
                m2 = dve_tt(norm[:, t, :].rearrange("p (h d) -> p h d", d=D), heads[:, :, 0:D],
                            rc[:, :].unsqueeze(2).broadcast_to([P, H, D]), ALU.mult, "dve_norm")
                bank_any.release(bi, m2)
                recip_ring.release(ri, m2)
            osum_ring.release(osum["index"], m)
            yield
            res = {}
            yield from bank_to_split(res)
            bi, bank, bfree = bank_any.take()
            wait("pe", m2, *bfree)
            for c in range(CC):
                for t in range(LT):
                    m = turn(bank[:, c * L + t * P:c * L + (t + 1) * P], norm[:, t, c * P:(c + 1) * P],
                             "pe_turn" if (c, t) == (CC - 1, LT - 1) else None)
            norm_ring.release(ni, m)
            yield from split(bi, bank, m, None, res)
            yield from held(bank_any)
            bi, bank, bfree = bank_any.take()
            wait("pe", *res["marks"], w["mark"], *bfree)
            for c in range(CC):
                m = project(bank[:, c * L:(c + 1) * L], w, slice(c * P, (c + 1) * P), res["pair"], CC, "pe_out")
            pair_ring.release(res["index"], m)
            yield
            yield from add_rows(bi, bank, m, scale, shift, X, result)

        def add_rows(bi, bank, mark, scale, shift, X, result):
            yield from held(full_ring)
            fi, full, ffree = full_ring.take()
            wait("act", mark, *ffree)
            for c in range(CC):
                kw = dict(bias=shift(c)) if scale is None else dict(scale=scale(c), bias=shift(c))
                m = act(full[:, c, :], bank[:, c * L:(c + 1) * L], ACT.Identity, "act_out", **kw)
            bank_any.release(bi, m)
            yield
            yield from held(bank_any)
            bi, bank, bfree = bank_any.take()
            wait("pe", m, *bfree)
            for t in range(LT):
                for c in range(CC):
                    m = turn(bank[:, t * C + c * P:t * C + (c + 1) * P], full[:, c, t * P:(t + 1) * P],
                             "pe_turn" if (c, t) == (CC - 1, LT - 1) else None)
            full_ring.release(fi, m)
            yield
            wait("dve", m, *result["marks"])
            m = dve_tt(X[:, :, :], X[:, :, :], bank[:, :].rearrange("p (t c) -> p t c", t=LT), ALU.add, "dve_x")
            bank_any.release(bi, m)
            result["marks"] = [m]
            yield

        x_of, after_self, after_top, after_mlp, top_slot, top_osum = {}, {}, {}, {}, {}, {}

        def roll_copy(b, tile, load, signal, src=None):
            dram = A["x"] if load else out
            for rows, at in ((slice(SHIFT, SHIFT + P), tile[:, 0, :]),
                             (slice(SHIFT + P, L), tile[0:L - SHIFT - P, 1, :]),
                             (slice(0, SHIFT), tile[L - SHIFT - P:P, 1, :])):
                m = dma(at, dram[b, rows, :], signal) if load else dma(dram[b, rows, :], at, signal)
            return m

        def ada_at(i, b, src=ada):
            return lambda c: src[:, 2 * i + c, b:b + 1]

        def first_part():
            for b in range(B):
                yield from held(X_ring)
                xi, X, xfree = X_ring.take()
                wait("sp", *xfree)
                m = roll_copy(b, X, True, f"x_in{xi}")
                x_of[b] = dict(index=xi, tile=X, marks=[m])
                xs = x_of[b]
                while "ada" not in prog.marks:
                    yield
                wait("act", prog.marks["ada"], prog.marks["bias"])
                yield
                h = {}
                yield from layer_norm(X, xs["marks"], ada_at(1, b), ada_at(0, b), 1e-6, h)
                yield from held(stacks["self"])
                ki, slot, _ = stacks["self"].take()
                w = W["qkv"]
                yield from project_stack(w, 0, 0, True, 0, h["pair"], h["marks"], slot, "q")
                yield from project_stack(w, C, bias_at["qkv"] + CC, False, 0, h["pair"], h["marks"], slot, "k")
                yield from project_values(w, 2 * C, h["pair"], h["marks"], value_bias["self"], slot,
                                          slot.get("free", []))
                pair_ring.release(h["index"], slot["v_read"])
                for _ in range(4):
                    yield
                yield from held(osum_ring)
                oi, ot, ofree = osum_ring.take()
                osum = dict(index=oi, tile=ot, free=ofree)
                yield from attend(slot, True, osum)
                stacks["self"].release(ki)
                yield from finish_attention(osum, W["so"], ada_at(2, b),
                                            lambda c, b=b: gate_bias[:, c, b:b + 1], X, xs)
                h = {}
                yield from layer_norm(X, xs["marks"], ada_at(4, b), ada_at(3, b), 1e-6, h)
                yield from held(stacks["top"])
                ki, slot, _ = stacks["top"].take()
                yield from project_stack(W["q"], 0, 0, True, 1, h["pair"], h["marks"], slot, "q")
                pair_ring.release(h["index"], slot["pair_read"])
                yield from held(ctx_ring)
                ci, ct, cfree = ctx_ring.take()
                wait("sp", *cfree)
                cm = dma(ct[:, :, :], A["ctx_1024"][b].rearrange("(t p) c -> p t c", p=P), f"ctx_in{ci}")
                yield
                yield
                c_pair = {}
                yield from bank_to_split(c_pair)
                bi, bank, bfree = bank_any.take()
                wait("pe", cm, *bfree)
                for c in range(CC):
                    for t in range(LT):
                        m = turn(bank[:, c * L + t * P:c * L + (t + 1) * P], ct[:, t, c * P:(c + 1) * P],
                                 "pe_turn" if (c, t) == (CC - 1, LT - 1) else None)
                ctx_ring.release(ci, m)
                yield from split(bi, bank, m, None, c_pair)
                yield from project_stack(W["kv"], 0, bias_at["kv"], False, 0, c_pair["pair"], c_pair["marks"],
                                         slot, "k")
                yield from project_values(W["kv"], C, c_pair["pair"], c_pair["marks"], value_bias["top"], slot,
                                          slot.get("free", []))
                pair_ring.release(c_pair["index"], slot["v_read"])
                slot["ring_index"] = ki
                top_slot[b] = slot
                yield

        def top_part():
            waiting = []

            def close(entry):
                b, g, far, done, osum, slot = entry
                m = attend_group(slot, osum, g, False, far, [done["mark"]])
                if g == NG - 1:
                    slot["free"] = [m]
                    stacks["top"].release(slot["ring_index"])
                    top_osum[b] = osum

            for b in range(B):
                while b not in top_slot:
                    if waiting and bank_out.ready() and bank_prob.ready() and prob_ring.ready():
                        close(waiting.pop(0))
                    yield
                slot = top_slot[b]
                q, k = slot["q"], slot["k"]
                osum = None
                for g in range(NG):
                    yield from held(rowmax_ring)
                    ri, rm, rfree = rowmax_ring.take()
                    far = []
                    for hj in range(G4):
                        h = g * G4 + hj
                        yield from held(bank_score)
                        bi, bank, bfree = bank_score.take()
                        wait("pe", slot["q_mark"], slot["k_mark"], *bfree)
                        for t in range(LT):
                            m = mm(bank[:, t * L:(t + 1) * L], q[0:NR, h, t * P:(t + 1) * P], k[0:NR, h, :],
                                   True, True, "pe_top")
                        for r in (best_ring, far_ring):
                            yield from held(r)
                        e8, best, efree = best_ring.take()
                        fi, ftile, ffree = far_ring.take()
                        rests = []
                        for t in range(LT):
                            yield from held(rest_ring)
                            rests.append(rest_ring.take())
                        yield
                        wait("dve", m, *rfree, *efree, *ffree)
                        top8 = [dve_max8(rm[:, hj, t, :], bank[:, t * L:(t + 1) * L], "dve_top")
                                for t in range(LT)]
                        yield
                        part = []
                        for t in range(LT):
                            wait("dve", top8[t], *rests[t][2])
                            part.append(dve_replace(rests[t][1][:, :], rm[:, hj, t, :],
                                                    bank[:, t * L:(t + 1) * L], "dve_top"))
                        bank_score.release(bi, part[-1])
                        yield
                        for t in range(LT):
                            wait("dve", part[t])
                            top8[t] = dve_max8(best[:, t, :], rests[t][1][:, :], "dve_top")
                        yield
                        for t in range(LT):
                            wait("dve", top8[t])
                            m = dve_replace(ftile[:, t, :], best[:, t, :], rests[t][1][:, :], "dve_top")
                            rest_ring.release(rests[t][0], m)
                        best_ring.release(e8, m)
                        wait("pool", m)
                        m2 = pool_ts(ftile[:, :, :], ftile[:, :, :], FAR, -1.0, ALU.add, ALU.mult, "pool_far")
                        far.append((fi, ftile, m2))
                        if hj == 1 and waiting:
                            while not (bank_out.ready() and bank_prob.ready() and prob_ring.ready()):
                                yield
                            close(waiting.pop(0))
                        yield
                    if g == 0:
                        yield from held(osum_ring)
                        oi, ot, ofree = osum_ring.take()
                        osum = dict(index=oi, tile=ot, free=ofree)
                    done = {}
                    yield from guard(slot, rm, g * G4, G4, m, done)
                    rowmax_ring.release(ri, done["mark"])
                    waiting.append((b, g, far, done, osum, slot))
            while waiting:
                for _ in range(8):
                    yield
                while not (bank_out.ready() and bank_prob.ready() and prob_ring.ready()):
                    yield
                close(waiting.pop(0))

        def mlp_part():
            for b in range(B):
                while b not in top_osum:
                    yield
                xs = x_of[b]
                X = xs["tile"]
                yield from finish_attention(top_osum[b], W["co"], ada_at(5, b),
                                            lambda c, b=b: gate_bias[:, CC + c, b:b + 1], X, xs)
                h = {}
                yield from layer_norm(X, xs["marks"], ada_at(7, b), ada_at(6, b), 1e-6, h)
                yield from split_in(W["m2"])
                yield from held(hid_ring)
                hi_, hid, hfree = hid_ring.take()
                marks = []
                for n2 in range(0, HC, 2):
                    yield from held(gated_ring)
                    gi, gated, gfree = gated_ring.take()
                    for n in range(n2, n2 + 2):
                        yield from held(bank_any, tanh_ring)
                        bi, bank, bfree = bank_any.take()
                        ti, th, tfree = tanh_ring.take()
                        wait("pe", *h["marks"], W["m1"]["mark"], *bfree)
                        project(bank[:, 0:L], W["m1"], slice(n * P, (n + 1) * P), h["pair"], CC, None)
                        m = project(bank[:, L:2 * L], W["m1"], slice(HID + n * P, HID + (n + 1) * P), h["pair"],
                                    CC, "pe_mlp")
                        h["read"] = m
                        yield
                        wait("act", m, *tfree)
                        t = act(th[:, 0, :], bank[:, 0:L], ACT.Tanh, "act_tanh", scale=0.5,
                                bias=half_bias[:, n:n + 1])
                        wait("pool", t)
                        t = pool_ts(th[:, 1, :], th[:, 0, :], 1.0, 1.0, ALU.add, ALU.mult, "pool_tanh")
                        yield
                        at = bias_at["m1"] + n
                        wait("dve", t, *gfree)
                        t = dve_stt(th[:, 0, :], bank[:, 0:L], bias_col[:, at:at + 1], th[:, 1, :], ALU.add,
                                    ALU.mult, "dve_mlp")
                        yield
                        wait("dve", t)
                        t = dve_stt(gated[:, n - n2, :], bank[:, L:2 * L], bias_col[:, at + HC:at + HC + 1],
                                    th[:, 0, :], ALU.add, ALU.mult, "dve_mlp")
                        bank_any.release(bi, t)
                        tanh_ring.release(ti, t)
                    yield
                    wait("act", t, *hfree)
                    m1 = act(hid[:, 0, n2:n2 + 2, :], gated[:, :, :], ACT.Copy, "act_split")
                    wait("pool", m1, *hfree)
                    m2 = pool_tt(hid[:, 1, n2:n2 + 2, :], gated[:, :, :], hid[:, 0, n2:n2 + 2, :], ALU.subtract,
                                 "pool_split")
                    gated_ring.release(gi, m2)
                    marks = [m1, m2]
                pair_ring.release(h["index"], h["read"])
                yield
                yield
                yield from held(bank_any)
                bi, bank, bfree = bank_any.take()
                wait("pe", *marks, W["m2"]["mark"], *bfree)
                for c in range(CC):
                    m = project(bank[:, c * L:(c + 1) * L], W["m2"], slice(c * P, (c + 1) * P), hid, HC, "pe_mlp")
                hid_ring.release(hi_, m)
                yield
                yield from add_rows(bi, bank, m, lambda c, b=b: half_gate[:, c, b:b + 1],
                                    lambda c, b=b: gate_bias[:, 2 * CC + c, b:b + 1], X, xs)
                after_mlp[b] = True

        def last_part():
            while "ada" not in prog.marks:
                yield
            for b in range(B):
                while b not in top_slot:
                    yield
                yield from held(stacks["last"])
                ki, slot, _ = stacks["last"].take()
                yield from held(ctx_ring)
                ci, ct, cfree = ctx_ring.take()
                wait("sp", *cfree)
                cm = dma(ct[:, :, :], A["ctx_1024"][b].rearrange("(t p) c -> p t c", p=P), f"ctx_in{ci}")
                yield
                yield
                h = {}
                yield from layer_norm(ct, [cm], ada_at(0, b, sskv), ada_at(1, b, sskv), 1e-5, h)
                ctx_ring.release(ci, h["read"])
                yield from project_stack(W["Wkv"], 0, bias_at["bkv"], False, 0, h["pair"], h["marks"], slot, "k")
                yield from project_values(W["Wkv"], C, h["pair"], h["marks"], value_bias["last"], slot,
                                          slot.get("free", []))
                pair_ring.release(h["index"], slot["v_read"])
                while b not in after_mlp:
                    yield
                xs = x_of[b]
                X = xs["tile"]
                h = {}
                yield from layer_norm(X, xs["marks"], ada_at(0, b, ssq), ada_at(1, b, ssq), 1e-5, h)
                yield from project_stack(W["Wq"], 0, 0, True, 2, h["pair"], h["marks"], slot, "q")
                pair_ring.release(h["index"], slot["pair_read"])
                for _ in range(4):
                    yield
                yield from held(osum_ring)
                oi, ot, ofree = osum_ring.take()
                osum = dict(index=oi, tile=ot, free=ofree)
                yield from attend(slot, False, osum)
                stacks["last"].release(ki)
                yield from finish_attention(osum, W["Wp"], None,
                                            lambda c: bias_col[:, bias_at["bp"] + c:bias_at["bp"] + c + 1], X, xs)
                wait("sp", *xs["marks"])
                m = roll_copy(b, X, False, f"x_out{xs['index']}")
                X_ring.release(xs["index"], m)

        pre = prologue()
        parts = [pre, top_part(), first_part(), mlp_part(), last_part()]
        idle = 0
        while parts:
            before = sum(len(v) for v in prog.queue.values())
            for p in list(parts):
                try:
                    next(p)
                except StopIteration:
                    parts.remove(p)
            idle = idle + 1 if before == sum(len(v) for v in prog.queue.values()) else 0
            assert idle < 200, "no part can go on"
        for name, n in prog.count.items():
            if name[:3] in ("to_", "x_o"):
                wait("sp", (name, n))

        block = ctx.enter_context(nc.Block())

        @block.sync
        def _(eng):
            for f in prog.queue["sp"]:
                f(eng)

        @block.tensor
        def _(eng):
            for f in prog.queue["pe"]:
                f(eng)

        @block.scalar
        def _(eng):
            for f in prog.queue["act"]:
                f(eng)

        @block.vector
        def _(eng):
            for f in prog.queue["dve"]:
                f(eng)

        @block.gpsimd
        def _(eng):
            for f in prog.queue["pool"]:
                f(eng)


def kernel(**inputs):
    import numpy as np
    import concourse.bacc as bacc
    from concourse.bass_utils import run_bass_kernel_spmd

    nc = bacc.Bacc("TRN2", target_bir_lowering=False, num_devices=1)
    arrays, aps = {}, {}
    for name, value in inputs.items():
        a = np.ascontiguousarray(value)
        arrays[f"in_{name}"] = a
        aps[name] = nc.dram_tensor(f"in_{name}", a.shape, mybir.dt.from_np(a.dtype), kind="ExternalInput").ap()
    shape = inputs["x"].shape
    out = nc.dram_tensor("out_x", shape, F32, kind="ExternalOutput").ap()
    build(nc, aps, out)
    r = run_bass_kernel_spmd(nc, [arrays], core_ids=[0])
    return r.results[0]["out_x"]
```

```python
from contextlib import ExitStack

import concourse.bass as bass
import concourse.mybir as mybir

F32 = mybir.dt.float32
F16 = mybir.dt.float16
BF16 = mybir.dt.bfloat16
ALU = mybir.AluOpType
ACT = mybir.ActivationFunctionType
AX = mybir.AxisListType

P = 128
SLOT = 32
PE_NS = 0.55
FAR = 2.0 ** 100


class Program:

    TAIL = {"sp": 2000.0, "pe": 330.0, "act": 180.0, "dve": 160.0, "pool": 120.0}

    def __init__(self, nc, ctx):
        self.nc, self.ctx = nc, ctx
        self.queue = {"sp": [], "pe": [], "act": [], "dve": [], "pool": []}
        self.waited = {e: {} for e in self.queue}
        self.count, self.sems, self.marks = {}, {}, {}
        self.clock = {e: 0.0 for e in self.queue}
        self.busy = {e: 0.0 for e in self.queue}
        self.done = {}
        self.step_end = 0.0
        self.now = 0.0
        self.parts = []

    def sem(self, name):
        if name not in self.sems:
            self.sems[name] = self.ctx.enter_context(self.nc.semaphore(name))
            self.count[name] = 0
        return self.sems[name]

    def op(self, engine, emit, signal=None, by=1, ns=60.0, after=0.0):
        self.clock[engine] += ns
        self.busy[engine] += ns
        end = self.clock[engine] + self.TAIL[engine] + after
        self.step_end = max(self.step_end, end)
        if signal is None:
            self.queue[engine].append(emit)
            return None
        s = self.sem(signal)
        self.count[signal] += by
        self.done[signal, self.count[signal]] = end
        self.queue[engine].append(lambda e: emit(e).then_inc(s, by))
        return (signal, self.count[signal])

    def wait(self, engine, *marks):
        for mark in marks:
            name, value = mark
            self.clock[engine] = max(self.clock[engine], self.done[mark])
            if self.waited[engine].get(name, 0) >= value:
                continue
            self.waited[engine][name] = value
            s = self.sems[name]
            self.queue[engine].append(lambda e, s=s, v=value: e.wait_ge(s, v))


class Ring:

    def __init__(self, tiles, done):
        self.done = done
        self.tiles, self.free = tiles, [[] for _ in tiles]
        self.idle = list(range(len(tiles)))
        self.free_at = [0.0] * len(tiles)

    def ready(self):
        return bool(self.idle)

    def take(self):
        i = min(self.idle, key=lambda j: self.free_at[j])
        self.idle.remove(i)
        return i, self.tiles[i], self.free[i]

    def release(self, i, *marks):
        self.idle.append(i)
        self.free_at[i] = max([self.done[m] for m in marks], default=0.0)
        self.free[i] = list(marks)


def build(nc, A, out):
    B, L, C = A["x"].shape
    H = 16
    D = C // H
    TOP = 16
    SHIFT = 64
    HID = A["L0_xcond_w_m2"].shape[0]
    CC = C // P
    LT = L // P
    HC = HID // P
    G4 = P // SLOT
    NG = H // G4
    assert (CC, LT, NG, D) == (2, 2, 4, 16) and TOP == 16 and SHIFT * 2 == P
    QSCALE = float(D) ** -0.5

    with ExitStack() as ctx:
        prog = Program(nc, ctx)
        op, wait = prog.op, prog.wait

        def sb(name, shape, dt):
            return ctx.enter_context(nc.sbuf_tensor(name, shape, dt))

        def ring(name, n, shape, dt):
            return Ring([sb(f"{name}{i}", shape, dt) for i in range(n)], prog.done)

        def psum(name, n):
            return Ring([ctx.enter_context(nc.psum_tensor(f"{name}{i}", [P, 512], F32)) for i in range(n)], prog.done)

        bank_out = psum("bank_out", 1)
        bank_any = psum("bank_any", 7)

        ident32 = sb("ident32", [P, P], F32)
        ident16 = sb("ident16", [P, P], BF16)
        ones_row = sb("ones_row", [1, P], F16)
        minus_half = sb("minus_half", [P, LT], F32)

        NB = {"ada": 18, "qkv": 6, "so": 2, "q": 2, "kv": 4, "co": 2, "m1": 16, "m2": 2,
              "bq": 2, "bkv": 4, "bp": 2, "ssq": 4, "sskv": 4}
        bias_src = {"ada": "L0_xcond_b_ada", "qkv": "L0_xcond_b_qkv", "so": "L0_xcond_b_so",
                    "q": "L0_xcond_b_q", "kv": "L0_xcond_b_kv", "co": "L0_xcond_b_co",
                    "m1": "L0_xcond_b_m1", "m2": "L0_xcond_b_m2", "bq": "L1_xcond_bq",
                    "bkv": "L1_xcond_bkv", "bp": "L1_xcond_bp", "ssq": "L1_xcond_bss_q",
                    "sskv": "L1_xcond_bss_kv"}
        bias_at, rows = {}, 0
        for name, n in NB.items():
            bias_at[name] = rows
            rows += n
        NBR = rows
        bias_rows = sb("bias_rows", [NBR, P], F32)
        bias_col = sb("bias_col", [P, NBR], F32)
        q_bias = sb("q_bias", [P, 3 * CC], F32)
        half_bias = sb("half_bias", [P, HC], F32)

        W = {}
        for name, src, k, n, scale in (
            ("qkv", "L0_xcond_w_qkv", CC, 3 * C, 1.0), ("so", "L0_xcond_w_so", CC, C, 1.0),
            ("q", "L0_xcond_w_q", CC, C, QSCALE), ("kv", "L0_xcond_w_kv", CC, 2 * C, 1.0),
            ("co", "L0_xcond_w_co", CC, C, 1.0), ("m1", "L0_xcond_w_m1", CC, 2 * HID, 1.0),
            ("m2", "L0_xcond_w_m2", HC, C, 1.0), ("Wq", "L1_xcond_Wq", CC, C, QSCALE),
            ("Wkv", "L1_xcond_Wkv", CC, 2 * C, 1.0), ("Wp", "L1_xcond_Wp", CC, C, 1.0),
        ):
            W[name] = dict(src=A[src].rearrange("(k p) n -> p k n", p=P), k=k, n=n, scale=scale,
                           hi=sb(f"w_{name}_hi", [P, k, n], F16), lo=sb(f"w_{name}_lo", [P, k, n], F16))
        value_bias = {}
        for name, src, at in (("self", "L0_xcond_b_qkv", 2 * C), ("top", "L0_xcond_b_kv", C),
                              ("last", "L1_xcond_bkv", C)):
            value_bias[name] = dict(src=A[src][at:at + C].rearrange("(o n) -> o n", o=1),
                                    hi=sb(f"vb_{name}_hi", [1, C], F16),
                                    lo=sb(f"vb_{name}_lo", [1, C], F16))

        NA = NB["ada"]
        cond_T = sb("cond_T", [P, CC, B], F32)
        cond_t = sb("cond_t", [P, CC, B], F32)
        cond_s = sb("cond_s", [P, CC, B], F32)
        ada = sb("ada", [P, NA, B], F32)
        gate_bias = sb("gate_bias", [P, 3 * CC, B], F32)
        half_gate = sb("half_gate", [P, CC, B], F32)
        ssq = sb("ssq", [P, NB["ssq"], B], F32)
        sskv = sb("sskv", [P, NB["sskv"], B], F32)

        X_ring = ring("x_tile", 4, [P, LT, C], F32)
        ctx_ring = ring("ctx_tile", 2, [P, LT, C], F32)
        stats_ring = ring("stats", 4, [P, LT, 6], F32)
        mv_ring = ring("mean_var", 4, [P, LT, 2], F32)
        rstd_ring = ring("rstd", 4, [P, 3, LT], F32)
        norm_ring = ring("normed", 2, [P, LT, C], F32)
        full_ring = ring("full", 3, [P, CC, L], F32)
        pair_ring = ring("pair", 4, [P, 2, CC, L], F16)
        self_parts = ring("self_parts", 2, [P, 2, CC, L], F16)
        top_parts = ring("top_parts", 1, [P, 2, CC, L], F16)
        last_k_parts = ring("last_k_parts", 1, [P, 2, CC, L], F16)
        last_q_parts = ring("last_q_parts", 1, [P, 2, CC, L], F16)
        values = {kind: ring(f"v_{kind}", n, [P, LT, H, SLOT], F32) for kind, n in
                  (("self", 2), ("top", 2), ("last", 1))}
        tanh_ring = ring("tanh", 2, [P, 2, L], F32)
        gated_ring = ring("gated", 2, [P, 2, L], F32)
        hid_ring = ring("hid", 1, [P, 2, HC, L], F16)
        prob_ring = ring("prob", 3, [P, 512], F32)
        osum_ring = ring("osum", 3, [P, NG, L], F32)
        recip_ring = ring("recip", 4, [P, H], F32)
        rest_ring = ring("rest", 4, [P, L], F32)
        best_ring = ring("best", 4, [P, LT, 8], F32)
        far_ring = ring("far", 10, [P, LT, L], BF16)
        rowmax_ring = ring("rowmax", 3, [P, 8, LT, 8], F32)
        guard_ring = ring("guard", 3, [16, P], F16)

        NR = 3 * D
        PARTS = {"q": (0, 1, 0), "k": (0, 0, 1)}
        stacks, slots = {}, []
        for pair_of in (("top0", "top1"), ("self0", "last0")):
            halves = {w: sb(f"{w}_stack_{pair_of[0]}_{pair_of[1]}", [P, H, L], F16) for w in "qk"}
            for name, base in zip(pair_of, (0, P // 2)):
                slots.append(dict(
                    name=name, tile=halves, base=base,
                    q=halves["q"][base:base + NR + 1, :, :], k=halves["k"][base:base + NR + 1, :, :],
                    dq=nc.dram_tensor(f"dq_{name}", (2, C, L), F16, kind="Internal").ap(),
                    dk=nc.dram_tensor(f"dk_{name}", (2, C, L), F16, kind="Internal").ap(),
                    dm=nc.dram_tensor(f"dm_{name}", (H, LT, P), F16, kind="Internal").ap()))
        for kind in ("top", "self", "last"):
            stacks[kind] = Ring([s for s in slots if s["name"][:-1] == kind], prog.done)
        stage_cols = 4 * C
        stage = [sb(f"stage{i}", [P, stage_cols], F32) for i in range(2)]
        cond = stage[1][0:B, 0:C]
        for i, v in enumerate(value_bias.values()):
            v["raw"] = stage[1][0:1, (i + 1) * C:(i + 2) * C]

        def cols(o):
            return o.free_size()

        def mm(o, lhsT, rhs, start, stop, signal=None):
            passes = 4 if lhsT.dtype == F32 else 1
            if lhsT.dtype == F32 and lhsT.free_size() == SLOT:
                passes = 1
            return op("pe", lambda e: e.matmul(o, lhsT, rhs, start=start, stop=stop), signal,
                      ns=max(27.0, PE_NS * passes * cols(rhs)))

        def turn(o, i, signal=None):
            n = i.partition_size()
            return op("pe", lambda e: e.transpose(o, i, ident32[0:n, 0:n]), signal, ns=PE_NS * n)

        def act(o, i, f, signal=None, **kw):
            return op("act", lambda e: e.activation(o, i, f, **kw), signal, ns=70 + cols(i) / 1.2)

        def dma(o, i, signal):
            return op("sp", lambda e: e.dma_start(o, i), signal, 16, ns=60.0, after=600.0)

        def dve(o, emit, signal=None, n=None):
            return op("dve", emit, signal, ns=((n or cols(o)) + 66) / 0.96)

        def dve_tt(o, a, b, f, signal=None):
            return dve(o, lambda e: e.tensor_tensor(o, a, b, f), signal)

        def dve_ts(o, a, s1, s2, f0, f1, signal=None):
            return dve(o, lambda e: e.tensor_scalar(o, a, s1, s2, f0, f1), signal)

        def dve_stt(o, a, s, b, f0, f1, signal=None):
            return dve(o, lambda e: e.scalar_tensor_tensor(o, a, s, b, f0, f1), signal)

        def dve_max8(o, i, signal):
            return dve(o, lambda e: e.max(o, i), signal, cols(i))

        def dve_replace(o, what, i, signal):
            return dve(o, lambda e: e.match_replace(o, what, i, -FAR), signal)

        def dve_rowmax(o, i, signal):
            return dve(o, lambda e: e.tensor_reduce(o, i, AX.X, ALU.max), signal, cols(i))

        def dve_reciprocal(o, i, signal):
            return dve(o, lambda e: e.reciprocal(o, i), signal)

        def pool_tt(o, a, b, f, signal=None):
            per = 165.0 if f == ALU.pow else 1.95
            return op("pool", lambda e: e.tensor_tensor(o, a, b, f), signal, ns=150 + per * cols(o))

        def pool_ts(o, a, s1, s2, f0, f1, signal=None):
            return op("pool", lambda e: e.tensor_scalar(o, a, s1, s2, f0, f1), signal,
                      ns=(300 if cols(o) == L else 160) + cols(o) / 1.2)

        def prologue():
            marks = prog.marks
            z = op("pool", lambda e: e.memset(ident32[:, :], 0.0), "const")
            z = op("pool", lambda e: e.memset(ident16[:, :], 0.0), "const")
            wait("pool", z)
            for t in (ident32, ident16):
                one = op("pool", lambda e, t=t: e.affine_select(
                    out=t[:, :], in_=t[:, :], compare_op=ALU.not_equal, fill=1.0, base=0,
                    pattern=[[-1, P]], channel_multiplier=1), "const")
            marks["const"] = one
            op("dve", lambda e: e.memset(ones_row[:, :], 1.0), "const_dve")
            op("dve", lambda e: e.memset(minus_half[:, :], -0.5), "const_dve")
            for kind in stacks:
                for s in stacks[kind].tiles:
                    lo = s["base"] + SLOT
                    op("dve", lambda e, s=s, lo=lo: e.memset(s["tile"]["k"][lo:lo + SLOT, :, :], 1.0), "const_dve")
            for v in [v for r in values.values() for v in r.tiles]:
                marks["const2"] = op("dve", lambda e, v=v: e.memset(v[:, :, :, D:SLOT], 1.0), "const_dve")
            for name, src in bias_src.items():
                at = bias_at[name]
                m = dma(bias_rows[at:at + NB[name], :], A[src].rearrange("(m p) -> m p", p=P), "small_in")
            for v in value_bias.values():
                m = dma(v["raw"], v["src"], "small_in")
            m = dma(cond, A["cond_1024"], "small_in")
            wait("pe", marks["const"], m)
            i, bank, _ = bank_any.take()
            turn(bank[:, 0:NBR], bias_rows[:, :])
            for c in range(CC):
                t = turn(bank[:, 128 + B * c:128 + B * (c + 1)], cond[:, c * P:(c + 1) * P], "pe_pre")
            marks["cond_read"] = t
            wait("act", t)
            act(bias_col[:, :], bank[:, 0:NBR], ACT.Copy)
            cT = bank[:, 128:128 + CC * B].rearrange("p (c b) -> p c b", c=CC)
            act(cond_T[:, :, :], cT, ACT.Copy)
            t = act(cond_t[:, :, :], cT, ACT.Tanh, "act_pre", scale=0.5)
            bank_any.release(i, t)
            wait("dve", t, m)
            t = dve_stt(cond_s[:, :, :], cond_t[:, :, :], 1.0, cond_T[:, :, :], ALU.add, ALU.mult, "dve_pre")
            wait("dve", t)
            t = dve_ts(cond_T[:, :, :], cond_s[:, :, :], 0.5, None, ALU.mult, ALU.bypass, "dve_pre")
            marks["cond"] = t
            for j, name in enumerate(("qkv", "q", "bq")):
                dve_ts(q_bias[:, CC * j:CC * (j + 1)], bias_col[:, bias_at[name]:bias_at[name] + CC],
                       QSCALE, None, ALU.mult, ALU.bypass)
            marks["bias"] = dve_ts(half_bias[:, :], bias_col[:, bias_at["m1"]:bias_at["m1"] + HC], 0.5, None,
                                   ALU.mult, ALU.bypass, "dve_pre")
            for v in value_bias.values():
                op("dve", lambda e, v=v: e.tensor_copy(v["hi"][:, :], v["raw"]), "dve_pre")
            wait("dve", ("dve_pre", prog.count["dve_pre"]))
            for v in value_bias.values():
                marks["vbias"] = dve_tt(v["lo"][:, :], v["raw"], v["hi"][:, :], ALU.subtract, "dve_pre")
            yield
            stage_free = [[], [marks["cond_read"], marks["vbias"]]]
            turn_no = [0]

            def staged(src, k, n):
                i = turn_no[0] % 2
                turn_no[0] += 1
                wait("sp", *stage_free[i])
                view = stage[i][:, 0:k * n].rearrange("p (k n) -> p k n", k=k)
                return i, view, dma(view, src, f"stage_in{i}")

            for dst, src, bias, total in ((ada, "L0_xcond_w_ada", "ada", NA), (ssq, "L1_xcond_Wss_q", "ssq", 4),
                                          (sskv, "L1_xcond_Wss_kv", "sskv", 4)):
                for m0 in range(0, total, 4):
                    n = min(4, total - m0)
                    si, view, landed = staged(
                        A[src].rearrange("(k p) n -> p k n", p=P)[:, :, m0 * P:(m0 + n) * P], CC, n * P)
                    i, bank, free = bank_any.take()
                    wait("pe", landed, marks["cond"], *free)
                    for m in range(n):
                        for c in range(CC):
                            t = mm(bank[:, m * B:(m + 1) * B], view[:, c, m * P:(m + 1) * P], cond_T[:, c, :],
                                   c == 0, c == CC - 1, "pe_pre" if (m, c) == (n - 1, CC - 1) else None)
                    stage_free[si] = [t]
                    at = bias_at[bias] + m0
                    wait("dve", t)
                    t = dve_tt(dst[:, m0:m0 + n, :], bank[:, 0:n * B].rearrange("p (m b) -> p m b", b=B),
                               bias_col[:, at:at + n].unsqueeze(2).broadcast_to([P, n, B]), ALU.add, "dve_pre")
                    bank_any.release(i, t)
            wait("dve", t)
            for i in (1, 4, 7):
                dve_ts(ada[:, 2 * i:2 * i + 2, :], ada[:, 2 * i:2 * i + 2, :], 1.0, None, ALU.add, ALU.bypass)
            for s in (ssq, sskv):
                dve_ts(s[:, 0:2, :], s[:, 0:2, :], 1.0, None, ALU.add, ALU.bypass)
            dve_ts(half_gate[:, :, :], ada[:, 16:18, :], 0.5, None, ALU.mult, ALU.bypass)
            for j, name in enumerate(("so", "co", "m2")):
                g = 2 * (3 * j + 2)
                at = bias_at[name]
                marks["ada"] = dve_tt(gate_bias[:, CC * j:CC * (j + 1), :], ada[:, g:g + 2, :],
                                      bias_col[:, at:at + 2].unsqueeze(2).broadcast_to([P, CC, B]),
                                      ALU.mult, "dve_pre")
            for name in ("qkv", "so", "q", "kv", "co", "m1", "m2", "Wq", "Wkv", "Wp"):
                w = W[name]
                width = min(w["n"], stage_cols // w["k"] // P * P)
                for n0 in range(0, w["n"], width):
                    n = min(width, w["n"] - n0)
                    si, view, landed = staged(w["src"][:, :, n0:n0 + n], w["k"], n)
                    hi, lo = w["hi"][:, :, n0:n0 + n], w["lo"][:, :, n0:n0 + n]
                    parts = [(0, n, w["scale"])]
                    if name == "qkv":
                        parts = [(max(0, a - n0), min(n, b - n0), s) for a, b, s in
                                 ((0, C, QSCALE), (C, 3 * C, 1.0)) if max(n0, a) < min(n0 + n, b)]
                    wait("act", landed)
                    for a, b, s in parts:
                        t = act(hi[:, :, a:b], view[:, :, a:b], ACT.Copy, "act_pre", scale=s)
                    wait("dve", t)
                    for a, b, s in parts:
                        t = dve_stt(lo[:, :, a:b], view[:, :, a:b], s, hi[:, :, a:b], ALU.mult, ALU.subtract,
                                    "dve_pre")
                    stage_free[si] = [t]
                W[name]["mark"] = t
                yield
            for i in range(2):
                for j in range(0, stage_cols, LT * C):
                    X_ring.tiles.append(stage[i][:, j:j + LT * C].rearrange("p (t c) -> p t c", t=LT))
                    X_ring.free.append(None)
                    X_ring.free_at.append(0.0)
                    X_ring.release(len(X_ring.tiles) - 1, *stage_free[i])

        def held(*rings):
            while not all(r.ready() for r in rings):
                yield
            at = max(min(r.free_at[i] for i in r.idle) for r in rings)
            if at > prog.now:
                prog.step_end = max(prog.step_end, at)
                yield
                yield from held(*rings)

        def due(*marks):
            at = max(prog.done[m] for m in marks)
            if at > prog.now:
                prog.step_end = max(prog.step_end, at)
                yield

        def together(*steps):
            left = [len(steps)]

            def run(g):
                yield from g
                left[0] -= 1

            for g in steps:
                prog.parts.append([prog.now, run(g), False])
            while left[0]:
                yield

        def split_in(w):
            while "mark" not in w:
                yield

        def layer_norm(src, src_marks, scale, shift, eps, result):
            yield from due(*src_marks)
            yield from held(stats_ring, mv_ring, rstd_ring, norm_ring)
            si, stats, sfree = stats_ring.take()
            mi, mv, mfree = mv_ring.take()
            ri, rstd, rfree = rstd_ring.take()
            ni, norm, nfree = norm_ring.take()
            wait("dve", *src_marks, *sfree, *mfree)
            for t in range(LT):
                m = dve(None, lambda e, t=t: e.bn_stats(stats[:, t, :], src[:, t, :]), "dve_ln", C)
            yield
            wait("dve", m)
            for t in range(LT):
                m = dve(None, lambda e, t=t: e.bn_aggr(mv[:, t, :], stats[:, t, :]), "dve_ln", 26)
            stats_ring.release(si, m)
            yield
            wait("pool", m, prog.marks["const2"], *rfree, *nfree)
            m = pool_ts(rstd[:, 0, :], mv[:, :, 1], eps, 1.0, ALU.add, ALU.mult, "pool_ln")
            wait("pool", m)
            m = pool_tt(rstd[:, 1, :], rstd[:, 0, :], minus_half[:, :], ALU.pow, "pool_ln")
            wait("pool", m)
            m = pool_tt(rstd[:, 0, :], mv[:, :, 0], rstd[:, 1, :], ALU.mult, "pool_ln")
            wait("pool", m)
            m = pool_ts(rstd[:, 2, :], rstd[:, 0, :], -1.0, 0.0, ALU.mult, ALU.add, "pool_ln")
            mv_ring.release(mi, m)
            wait("pool", m)
            for t in range(LT):
                m = pool_ts(norm[:, t, :], src[:, t, :], rstd[:, 1, t:t + 1], rstd[:, 2, t:t + 1],
                            ALU.mult, ALU.add, "pool_ln")
            rstd_ring.release(ri, m)
            result["read"] = m
            yield
            yield
            yield from bank_to_split(result)
            bi, bank, bfree = bank_any.take()
            wait("pe", m, *bfree)
            for c in range(CC):
                for t in range(LT):
                    m = turn(bank[:, c * L + t * P:c * L + (t + 1) * P], norm[:, t, c * P:(c + 1) * P],
                             "pe_turn" if (c, t) == (CC - 1, LT - 1) else None)
            norm_ring.release(ni, m)
            yield from split(bi, bank, m, [(scale(c), shift(c)) for c in range(CC)], result)

        def bank_to_split(result, pairs=pair_ring):
            yield from held(bank_any, full_ring, pairs)
            result["full"], result["taken"], result["ring"] = full_ring.take(), pairs.take(), pairs

        def split(bi, bank, mark, affine, result):
            fi, full, ffree = result["full"]
            pi, pair, pfree = result["taken"]
            yield
            wait("act", mark, *ffree, *pfree)
            view = bank[:, :].rearrange("p (c l) -> p c l", c=CC)
            if affine is None:
                act(full[:, :, :], view, ACT.Copy)
                m = act(pair[:, 0, :, :], view, ACT.Copy, "act_split")
            else:
                for c, (s, b) in enumerate(affine):
                    kw = dict(bias=b) if s is None else dict(scale=s, bias=b)
                    act(full[:, c, :], view[:, c, :], ACT.Identity, **kw)
                    m = act(pair[:, 0, c, :], view[:, c, :], ACT.Identity, "act_split", **kw)
            bank_any.release(bi, m)
            yield
            wait("pool", m)
            m2 = pool_tt(pair[:, 1, :, :], full[:, :, :], pair[:, 0, :, :], ALU.subtract, "pool_split")
            full_ring.release(fi, m2)
            result.update(pair=pair, index=pi, marks=[m, m2])
            yield

        def project(bank_at, w, cols, pair, chunks, signal):
            for k in range(chunks):
                for n, (a, b) in enumerate((("hi", 0), ("hi", 1), ("lo", 0))):
                    last = k == chunks - 1 and n == 2
                    m = mm(bank_at, w[a][:, k, cols], pair[:, b, k, :], k == 0 and n == 0, last,
                           signal if last else None)
            return m

        def to_stack(slot, which, res):
            s, name, d = slot[which], slot["name"] + which, slot["d" + which]
            wait("sp", prog.marks["const2"], *res["marks"], *slot.get("free_d" + which, []))
            for part in range(2):
                m = dma(d[part].rearrange("(c p) l -> p c l", p=P), res["pair"][:, part, :, :], f"to_{name}")
            res["ring"].release(res["index"], m)
            wait("sp", m, *slot.get("free", []))
            for r, part in enumerate(PARTS[which]):
                m = dma(s[r * D:(r + 1) * D, :, :], d[part].rearrange("(h d) l -> d h l", d=D), f"from_{name}")
            slot["free_d" + which] = [m]
            slot[which + "_mark"] = m

        def project_values(w, col0, h, bias, ring, v):
            yield from split_in(w)
            yield from held(bank_any, ring)
            bi, bank, bfree = bank_any.take()
            v["ring"] = ring
            v["index"], v["tile"], vfree = ring.take()
            pair = h["pair"]
            wait("pe", *h["marks"], w["mark"], prog.marks["const2"], *bfree)
            for t in range(LT):
                o = bank[:, t * C:(t + 1) * C]
                mm(o, ones_row[:, :], bias["hi"][:, :], True, False)
                mm(o, ones_row[:, :], bias["lo"][:, :], False, False)
                for k in range(CC):
                    for n, (a, b) in enumerate(((0, "hi"), (1, "hi"), (0, "lo"))):
                        last = k == CC - 1 and n == 2
                        m = mm(o, pair[:, a, k, t * P:(t + 1) * P], w[b][:, k, col0:col0 + C], False, last,
                               "pe_v" if last and t == LT - 1 else None)
            h["reads"] = h.get("reads", []) + [m]
            yield
            wait("act", m, *vfree)
            v["mark"] = act(v["tile"][:, :, :, 0:D].rearrange("p t h d -> p (t h) d"),
                            bank[:, :].rearrange("p (g d) -> p g d", d=D), ACT.Copy, "act_v")
            bank_any.release(bi, v["mark"])

        def project_parts(w, col0, bias, h, pairs, res):
            yield from split_in(w)
            yield from bank_to_split(res, pairs)
            bi, bank, bfree = bank_any.take()
            wait("pe", *h["marks"], w["mark"], *bfree)
            for c in range(CC):
                m = project(bank[:, c * L:(c + 1) * L], w, slice(col0 + c * P, col0 + (c + 1) * P), h["pair"], CC,
                            "pe_qk")
            h["reads"] = h.get("reads", []) + [m]
            yield from split(bi, bank, m, [(None, bias(c)) for c in range(CC)], res)

        def query_bias(j):
            return lambda c: q_bias[:, CC * j + c:CC * j + c + 1]

        def key_bias(at):
            return lambda c: bias_col[:, at + c:at + c + 1]

        def guard(slot, rm, h0, n, mark, done):
            yield from held(bank_any, guard_ring)
            bi, bank, bfree = bank_any.take()
            gi, g, gfree = guard_ring.take()
            wait("pe", mark, *bfree)
            m = turn(bank[0:n * LT, 0:P], rm[:, 0:n, :, 0].rearrange("p h t -> p (h t)"), "pe_turn")
            yield
            wait("act", m, *gfree)
            m = act(g[0:n * LT, :], bank[0:n * LT, 0:P], ACT.Copy, "act_guard", scale=-1.0)
            bank_any.release(bi, m)
            name = slot["name"]
            wait("sp", m, *slot.get(("free_dm", h0), []))
            m = dma(slot["dm"][h0:h0 + n].rearrange("h t l -> (h t) l"), g[0:n * LT, :], f"to_m{name}_{h0}")
            guard_ring.release(gi, m)
            wait("sp", m, *slot.get("free", []))
            m = dma(slot["q"][NR:NR + 1, h0:h0 + n, :],
                    slot["dm"][h0:h0 + n].rearrange("(o h) t l -> o h (t l)", o=1), f"from_m{name}_{h0}")
            slot["free_dm", h0] = [m]
            done["mark"] = m
            yield

        def attend_group(slot, osum, g, window, far, marks):
            q, k, v = slot["q"], slot["k"], slot["v"]["tile"]
            step = 2 if window else 1
            todo = []
            yield from held(bank_out)
            out_bank = bank_out.take()
            for h0 in range(g * G4, (g + 1) * G4, step):
                yield from held(bank_any, prob_ring)
                bi, bank, bfree = bank_any.take()
                pi, prob, pfree = prob_ring.take()
                wait("pe", slot["v"]["mark"], slot["q_mark"], slot["k_mark"], prog.marks["const2"], *marks, *bfree)
                for h in range(h0, h0 + step):
                    for t in range(LT):
                        if window:
                            at = ((h - h0) * LT + t) * P
                            m = mm(bank[:, at:at + P], k[:, h, t * P:(t + 1) * P], q[:, h, t * P:(t + 1) * P],
                                   True, True, "pe_prob")
                            continue
                        o = bank[:, t * L:(t + 1) * L]
                        m = mm(o, k[:, h, t * P:(t + 1) * P], q[:, h, :], True, far is None,
                               "pe_prob" if far is None else None)
                        if far is not None:
                            fi, ftile, fmark = far[h % G4]
                            wait("pe", fmark)
                            for j in range(LT):
                                m = mm(o[:, j * P:(j + 1) * P], ftile[:, j, t * P:(t + 1) * P], ident16[:, :],
                                       False, j == LT - 1, "pe_prob" if j == LT - 1 else None)
                if far is not None:
                    far_ring.release(far[h0 % G4][0], m)
                wait("act", m, *pfree)
                e = act(prob[:, :], bank[:, :], ACT.Exp, "act_exp")
                bank_any.release(bi, e)
                todo.append((h0, pi, prob, e))
                yield
                if len(todo) == 2:
                    values_of(*todo.pop(0), window, step, g, out_bank, v)
            while todo:
                m = values_of(*todo.pop(0), window, step, g, out_bank, v)
                if todo:
                    yield
            oi, obank, _ = out_bank
            wait("act", m, *osum["free"])
            osum["mark"] = act(osum["tile"][:, g, :], obank[:, 0:L], ACT.Copy, "act_osum")
            bank_out.release(oi, osum["mark"])
            return m

        def values_of(h0, pi, prob, e, window, step, g, out_bank, v):
            _, obank, ofree = out_bank
            wait("pe", e, *ofree)
            for h in range(h0, h0 + step):
                j = (h - g * G4) * SLOT
                for t in range(LT):
                    if window:
                        m = mm(obank[j:j + SLOT, t * P:(t + 1) * P], v[:, t, h, :],
                               prob[:, ((h - h0) * LT + t) * P:((h - h0) * LT + t + 1) * P], True, True, "pe_pv")
                    else:
                        m = mm(obank[j:j + SLOT, 0:L], v[:, t, h, :], prob[:, t * L:(t + 1) * L],
                               t == 0, t == LT - 1, "pe_pv")
            prob_ring.release(pi, m)
            return m

        def row_maxima(slot, window, h8, done):
            q, k = slot["q"], slot["k"]
            yield from due(slot["q_mark"], slot["k_mark"])
            yield from held(rowmax_ring)
            ri, rm, rfree = rowmax_ring.take()
            step = 2 if window else 1
            for h0 in range(h8, h8 + 8, step):
                yield from held(bank_any)
                bi, bank, bfree = bank_any.take()
                wait("pe", slot["q_mark"], slot["k_mark"], *bfree)
                for h in range(h0, h0 + step):
                    for t in range(LT):
                        if window:
                            at = ((h - h0) * LT + t) * P
                            m = mm(bank[:, at:at + P], q[0:NR, h, t * P:(t + 1) * P],
                                   k[0:NR, h, t * P:(t + 1) * P], True, True, "pe_score")
                        else:
                            m = mm(bank[:, t * L:(t + 1) * L], q[0:NR, h, t * P:(t + 1) * P], k[0:NR, h, :],
                                   True, True, "pe_score")
                yield
                wait("dve", m, *rfree)
                m = dve_rowmax(rm[:, h0 - h8:h0 - h8 + step, :, 0],
                               bank[:, :].rearrange("p (h t k) -> p h t k", h=step, t=LT), "dve_max")
                bank_any.release(bi, m)
            d = {}
            yield
            yield from guard(slot, rm, h8, 8, m, d)
            rowmax_ring.release(ri, d["mark"])
            done[h8] = d["mark"]

        def attend(slot, window, osum):
            done = {}
            yield from together(*[row_maxima(slot, window, h8, done) for h8 in range(0, H, 8)])
            for g in range(NG):
                yield from due(done[g * G4 // 8 * 8])
                m = yield from attend_group(slot, osum, g, window, None, [done[g * G4 // 8 * 8]])
                yield
            slot["free"] = [m]
            slot["v"]["ring"].release(slot["v"]["index"], m)

        def finish_attention(osum, w, scale, shift, X, result):
            yield from split_in(w)
            yield from due(osum["mark"])
            yield from held(norm_ring)
            ni, norm, nfree = norm_ring.take()
            for t in range(LT):
                yield from held(bank_any, recip_ring)
                bi, bank, bfree = bank_any.take()
                ri, rc, rfree = recip_ring.take()
                wait("pe", osum["mark"], *bfree)
                for g in range(NG):
                    m = turn(bank[:, g * P:(g + 1) * P], osum["tile"][:, g, t * P:(t + 1) * P],
                             "pe_turn" if g == NG - 1 else None)
                yield
                heads = bank[:, :].rearrange("p (h s) -> p h s", s=SLOT)
                wait("dve", m, *rfree, *nfree)
                m2 = dve_reciprocal(rc[:, :], heads[:, :, D], "dve_norm")
                yield
                wait("dve", m2)
                m2 = dve_tt(norm[:, t, :].rearrange("p (h d) -> p h d", d=D), heads[:, :, 0:D],
                            rc[:, :].unsqueeze(2).broadcast_to([P, H, D]), ALU.mult, "dve_norm")
                bank_any.release(bi, m2)
                recip_ring.release(ri, m2)
            osum_ring.release(osum["index"], m)
            yield
            res = {}
            yield from bank_to_split(res)
            bi, bank, bfree = bank_any.take()
            wait("pe", m2, *bfree)
            for c in range(CC):
                for t in range(LT):
                    m = turn(bank[:, c * L + t * P:c * L + (t + 1) * P], norm[:, t, c * P:(c + 1) * P],
                             "pe_turn" if (c, t) == (CC - 1, LT - 1) else None)
            norm_ring.release(ni, m)
            yield from split(bi, bank, m, None, res)
            yield from held(bank_any)
            bi, bank, bfree = bank_any.take()
            wait("pe", *res["marks"], w["mark"], *bfree)
            for c in range(CC):
                m = project(bank[:, c * L:(c + 1) * L], w, slice(c * P, (c + 1) * P), res["pair"], CC, "pe_out")
            pair_ring.release(res["index"], m)
            yield
            yield from add_rows(bi, bank, m, scale, shift, X, result)

        def add_rows(bi, bank, mark, scale, shift, X, result):
            yield from held(full_ring)
            fi, full, ffree = full_ring.take()
            wait("act", mark, *ffree)
            for c in range(CC):
                kw = dict(bias=shift(c)) if scale is None else dict(scale=scale(c), bias=shift(c))
                m = act(full[:, c, :], bank[:, c * L:(c + 1) * L], ACT.Identity, "act_out", **kw)
            bank_any.release(bi, m)
            yield
            yield from held(bank_any)
            bi, bank, bfree = bank_any.take()
            wait("pe", m, *bfree)
            for t in range(LT):
                for c in range(CC):
                    m = turn(bank[:, t * C + c * P:t * C + (c + 1) * P], full[:, c, t * P:(t + 1) * P],
                             "pe_turn" if (c, t) == (CC - 1, LT - 1) else None)
            full_ring.release(fi, m)
            yield
            wait("dve", m, *result["marks"])
            m = dve_tt(X[:, :, :], X[:, :, :], bank[:, :].rearrange("p (t c) -> p t c", t=LT), ALU.add, "dve_x")
            bank_any.release(bi, m)
            result["marks"] = [m]
            yield

        projected, attended, x_of, top_keys, top_slot, top_osum, mlp_in = {}, {}, {}, {}, {}, {}, {}
        after_mlp, last_keys, last_query, last_osum = {}, {}, {}, {}
        top_scores, top_maxima, top_groups = [], [], []

        def roll_copy(b, tile, load, signal, src=None):
            dram = A["x"] if load else out
            for rows, at in ((slice(SHIFT, SHIFT + P), tile[:, 0, :]),
                             (slice(SHIFT + P, L), tile[0:L - SHIFT - P, 1, :]),
                             (slice(0, SHIFT), tile[L - SHIFT - P:P, 1, :])):
                m = dma(at, dram[b, rows, :], signal) if load else dma(dram[b, rows, :], at, signal)
            return m

        def ada_at(i, b, src=ada):
            return lambda c: src[:, 2 * i + c, b:b + 1]

        def load_part():
            for b in range(B):
                yield from held(X_ring)
                xi, X, xfree = X_ring.take()
                wait("sp", *xfree)
                m = roll_copy(b, X, True, f"x_in{xi}")
                x_of[b] = dict(index=xi, tile=X, marks=[m])
                yield
                while b - 1 not in projected and b > 0:
                    yield

        def self_part():
            while "ada" not in prog.marks:
                yield
            wait("act", prog.marks["ada"], prog.marks["bias"])
            for b in range(B):
                while b not in x_of:
                    yield
                xs = x_of[b]
                h = {}
                yield from layer_norm(xs["tile"], xs["marks"], ada_at(1, b), ada_at(0, b), 1e-6, h)
                w = W["qkv"]
                p = dict(q={}, k={}, v={})
                yield from together(
                    project_parts(w, 0, query_bias(0), h, self_parts, p["q"]),
                    project_parts(w, C, key_bias(bias_at["qkv"] + CC), h, self_parts, p["k"]),
                    project_values(w, 2 * C, h, value_bias["self"], values["self"], p["v"]))
                pair_ring.release(h["index"], *h["reads"])
                projected[b] = p
                yield

        def window_part():
            for b in range(B):
                while b not in projected:
                    yield
                yield from held(stacks["self"])
                ki, slot, _ = stacks["self"].take()
                p = projected[b]
                for which in "qk":
                    to_stack(slot, which, p[which])
                slot["v"] = p["v"]
                yield
                yield from held(osum_ring)
                oi, ot, ofree = osum_ring.take()
                osum = dict(index=oi, tile=ot, free=ofree)
                yield from attend(slot, True, osum)
                stacks["self"].release(ki)
                attended[b] = osum
                yield

        def query_part():
            for b in range(B):
                while b not in attended:
                    yield
                xs = x_of[b]
                X = xs["tile"]
                yield from finish_attention(attended[b], W["so"], ada_at(2, b),
                                            lambda c, b=b: gate_bias[:, c, b:b + 1], X, xs)
                h = {}
                yield from layer_norm(X, xs["marks"], ada_at(4, b), ada_at(3, b), 1e-6, h)
                while b not in top_keys:
                    yield
                slot = top_keys[b]
                q = {}
                yield from project_parts(W["q"], 0, query_bias(1), h, top_parts, q)
                pair_ring.release(h["index"], *h["reads"])
                to_stack(slot, "q", q)
                top_slot[b] = slot
                yield

        def load_context(b, cm):
            ci, ct, cfree = ctx_ring.take()
            wait("sp", *cfree)
            cm["mark"] = dma(ct[:, :, :], A["ctx_1024"][b].rearrange("(t p) c -> p t c", p=P), f"ctx_in{ci}")
            cm["index"], cm["tile"] = ci, ct

        def top_keys_part():
            while "bias" not in prog.marks:
                yield
            for b in range(B):
                yield from held(stacks["top"], ctx_ring)
                ki, slot, _ = stacks["top"].take()
                cm = {}
                load_context(b, cm)
                yield
                h, k, v = {}, {}, {}
                yield from bank_to_split(h)
                bi, bank, bfree = bank_any.take()
                wait("pe", cm["mark"], *bfree)
                for c in range(CC):
                    for t in range(LT):
                        m = turn(bank[:, c * L + t * P:c * L + (t + 1) * P], cm["tile"][:, t, c * P:(c + 1) * P],
                                 "pe_turn" if (c, t) == (CC - 1, LT - 1) else None)
                ctx_ring.release(cm["index"], m)
                yield from split(bi, bank, m, None, h)
                yield from together(
                    project_parts(W["kv"], 0, key_bias(bias_at["kv"]), h, top_parts, k),
                    project_values(W["kv"], C, h, value_bias["top"], values["top"], v))
                pair_ring.release(h["index"], *h["reads"])
                to_stack(slot, "k", k)
                slot["ring_index"], slot["v"] = ki, v
                top_keys[b] = slot
                yield

        def top_scores_part():
            for b in range(B):
                while b not in top_slot:
                    yield
                slot = top_slot[b]
                yield from due(slot["q_mark"], slot["k_mark"])
                q, k = slot["q"], slot["k"]
                for h in range(H):
                    while len(top_scores) > 1:
                        yield
                    yield from held(bank_any)
                    bi, bank, bfree = bank_any.take()
                    wait("pe", slot["q_mark"], slot["k_mark"], *bfree)
                    for t in range(LT):
                        m = mm(bank[:, t * L:(t + 1) * L], q[0:NR, h, t * P:(t + 1) * P], k[0:NR, h, :],
                               True, True, "pe_top")
                    top_scores.append((bi, bank, m))
                    yield

        def top_part():
            for b in range(B):
                for g in range(NG):
                    yield from held(rowmax_ring)
                    ri, rm, rfree = rowmax_ring.take()
                    far = []
                    for hj in range(G4):
                        yield from held(best_ring, far_ring)
                        while not top_scores:
                            yield
                        yield from due(top_scores[0][2])
                        bi, bank, m = top_scores.pop(0)
                        e8, best, efree = best_ring.take()
                        fi, ftile, ffree = far_ring.take()
                        rests = []
                        for t in range(LT):
                            yield from held(rest_ring)
                            rests.append(rest_ring.take())
                        wait("dve", m, *rfree, *efree, *ffree)
                        top8 = [dve_max8(rm[:, hj, t, :], bank[:, t * L:(t + 1) * L], "dve_top")
                                for t in range(LT)]
                        yield
                        part = []
                        for t in range(LT):
                            wait("dve", top8[t], *rests[t][2])
                            part.append(dve_replace(rests[t][1][:, :], rm[:, hj, t, :],
                                                    bank[:, t * L:(t + 1) * L], "dve_top"))
                        bank_any.release(bi, part[-1])
                        yield
                        for t in range(LT):
                            wait("dve", part[t])
                            top8[t] = dve_max8(best[:, t, :], rests[t][1][:, :], "dve_top")
                        yield
                        for t in range(LT):
                            wait("dve", top8[t])
                            m = dve_replace(ftile[:, t, :], best[:, t, :], rests[t][1][:, :], "dve_top")
                            rest_ring.release(rests[t][0], m)
                        best_ring.release(e8, m)
                        wait("pool", m)
                        m2 = pool_ts(ftile[:, :, :], ftile[:, :, :], FAR, -1.0, ALU.add, ALU.mult, "pool_far")
                        far.append((fi, ftile, m2))
                        yield
                    top_maxima.append((b, g, ri, rm, m, far))

        def top_guard_part():
            for _ in range(B * NG):
                while not top_maxima:
                    yield
                b, g, ri, rm, m, far = top_maxima.pop(0)
                yield from due(m)
                done = {}
                yield from guard(top_slot[b], rm, g * G4, G4, m, done)
                rowmax_ring.release(ri, done["mark"])
                top_groups.append((b, g, far, done["mark"]))

        def top_values_part():
            for _ in range(B * NG):
                while not top_groups:
                    yield
                b, g, far, mark = top_groups.pop(0)
                yield from due(mark)
                slot = top_slot[b]
                if g == 0:
                    yield from held(osum_ring)
                    oi, ot, ofree = osum_ring.take()
                    osum = dict(index=oi, tile=ot, free=ofree)
                m = yield from attend_group(slot, osum, g, False, far, [mark])
                if g == NG - 1:
                    slot["free"] = [m]
                    slot["v"]["ring"].release(slot["v"]["index"], m)
                    stacks["top"].release(slot["ring_index"])
                    top_osum[b] = osum
                yield

        def top_finish_part():
            for b in range(B):
                while b not in top_osum:
                    yield
                xs = x_of[b]
                X = xs["tile"]
                yield from finish_attention(top_osum[b], W["co"], ada_at(5, b),
                                            lambda c, b=b: gate_bias[:, CC + c, b:b + 1], X, xs)
                h = {}
                yield from layer_norm(X, xs["marks"], ada_at(7, b), ada_at(6, b), 1e-6, h)
                mlp_in[b] = h

        def mlp_part():
            for b in range(B):
                while b not in mlp_in:
                    yield
                xs, h = x_of[b], mlp_in[b]
                X = xs["tile"]
                yield from due(*h["marks"])
                yield from split_in(W["m2"])
                yield from held(hid_ring)
                hi_, hid, hfree = hid_ring.take()
                marks = []
                for n2 in range(0, HC, 2):
                    yield from held(gated_ring)
                    gi, gated, gfree = gated_ring.take()
                    for n in range(n2, n2 + 2):
                        yield from held(bank_any, tanh_ring)
                        bi, bank, bfree = bank_any.take()
                        ti, th, tfree = tanh_ring.take()
                        wait("pe", *h["marks"], W["m1"]["mark"], *bfree)
                        project(bank[:, 0:L], W["m1"], slice(n * P, (n + 1) * P), h["pair"], CC, None)
                        m = project(bank[:, L:2 * L], W["m1"], slice(HID + n * P, HID + (n + 1) * P), h["pair"],
                                    CC, "pe_mlp")
                        h["read"] = m
                        yield
                        wait("act", m, *tfree)
                        t = act(th[:, 0, :], bank[:, 0:L], ACT.Tanh, "act_tanh", scale=0.5,
                                bias=half_bias[:, n:n + 1])
                        wait("pool", t)
                        t = pool_ts(th[:, 1, :], th[:, 0, :], 1.0, 1.0, ALU.add, ALU.mult, "pool_tanh")
                        yield
                        at = bias_at["m1"] + n
                        wait("dve", t, *gfree)
                        t = dve_stt(th[:, 0, :], bank[:, 0:L], bias_col[:, at:at + 1], th[:, 1, :], ALU.add,
                                    ALU.mult, "dve_mlp")
                        yield
                        wait("dve", t)
                        t = dve_stt(gated[:, n - n2, :], bank[:, L:2 * L], bias_col[:, at + HC:at + HC + 1],
                                    th[:, 0, :], ALU.add, ALU.mult, "dve_mlp")
                        bank_any.release(bi, t)
                        tanh_ring.release(ti, t)
                    yield
                    wait("act", t, *hfree)
                    m1 = act(hid[:, 0, n2:n2 + 2, :], gated[:, :, :], ACT.Copy, "act_split")
                    wait("pool", m1, *hfree)
                    m2 = pool_tt(hid[:, 1, n2:n2 + 2, :], gated[:, :, :], hid[:, 0, n2:n2 + 2, :], ALU.subtract,
                                 "pool_split")
                    gated_ring.release(gi, m2)
                    marks = [m1, m2]
                pair_ring.release(h["index"], h["read"])
                yield
                yield
                yield from held(bank_any)
                bi, bank, bfree = bank_any.take()
                wait("pe", *marks, W["m2"]["mark"], *bfree)
                for c in range(CC):
                    m = project(bank[:, c * L:(c + 1) * L], W["m2"], slice(c * P, (c + 1) * P), hid, HC, "pe_mlp")
                hid_ring.release(hi_, m)
                yield
                yield from add_rows(bi, bank, m, lambda c, b=b: half_gate[:, c, b:b + 1],
                                    lambda c, b=b: gate_bias[:, 2 * CC + c, b:b + 1], X, xs)
                after_mlp[b] = True

        def last_keys_part():
            while "ada" not in prog.marks:
                yield
            for b in range(B):
                while b not in top_slot:
                    yield
                yield from held(ctx_ring, last_k_parts)
                cm = {}
                load_context(b, cm)
                yield
                h, k, v = {}, {}, {}
                yield from layer_norm(cm["tile"], [cm["mark"]], ada_at(0, b, sskv), ada_at(1, b, sskv), 1e-5, h)
                ctx_ring.release(cm["index"], h["read"])
                yield from together(
                    project_parts(W["Wkv"], 0, key_bias(bias_at["bkv"]), h, last_k_parts, k),
                    project_values(W["Wkv"], C, h, value_bias["last"], values["last"], v))
                pair_ring.release(h["index"], *h["reads"])
                last_keys[b] = k, v
                yield

        def last_query_part():
            for b in range(B):
                while b not in after_mlp:
                    yield
                yield from held(last_q_parts)
                xs = x_of[b]
                h, q = {}, {}
                yield from layer_norm(xs["tile"], xs["marks"], ada_at(0, b, ssq), ada_at(1, b, ssq), 1e-5, h)
                yield from project_parts(W["Wq"], 0, query_bias(2), h, last_q_parts, q)
                pair_ring.release(h["index"], *h["reads"])
                last_query[b] = q
                yield

        def last_part():
            for b in range(B):
                while b not in last_keys:
                    yield
                yield from held(stacks["last"])
                ki, slot, _ = stacks["last"].take()
                k, slot["v"] = last_keys[b]
                to_stack(slot, "k", k)
                yield
                while b not in last_query:
                    yield
                to_stack(slot, "q", last_query[b])
                yield
                yield from held(osum_ring)
                oi, ot, ofree = osum_ring.take()
                osum = dict(index=oi, tile=ot, free=ofree)
                yield from attend(slot, False, osum)
                stacks["last"].release(ki)
                last_osum[b] = osum

        def last_finish_part():
            for b in range(B):
                while b not in last_osum:
                    yield
                xs = x_of[b]
                X = xs["tile"]
                yield from finish_attention(last_osum[b], W["Wp"], None,
                                            lambda c: bias_col[:, bias_at["bp"] + c:bias_at["bp"] + c + 1], X, xs)
                wait("sp", *xs["marks"])
                m = roll_copy(b, X, False, f"x_out{xs['index']}")
                X_ring.release(xs["index"], m)

        parts = prog.parts
        parts += [[0.0, p, False] for p in (
            prologue(), top_part(), top_scores_part(), top_guard_part(), top_values_part(), load_part(), self_part(),
            window_part(), query_part(), top_keys_part(), top_finish_part(), mlp_part(), last_keys_part(),
            last_query_part(), last_part(), last_finish_part())]
        idle = 0
        while parts:
            parts.sort(key=lambda e: e[0])
            entry = parts[0]
            prog.step_end, prog.now = 0.0, entry[0]
            try:
                next(entry[1])
            except StopIteration:
                parts.remove(entry)
                continue
            if prog.step_end == 0.0:
                entry[2] = True
                entry[0] = max(entry[0], min([e[0] for e in parts if not e[2]], default=entry[0])) + 10.0
                idle += 1
                assert idle < 2000, "no part can go on"
            else:
                entry[0], idle = prog.step_end, 0
                entry[2] = False
        for name, n in prog.count.items():
            if name[:3] in ("to_", "x_o"):
                wait("sp", (name, n))

        block = ctx.enter_context(nc.Block())

        @block.sync
        def _(eng):
            for f in prog.queue["sp"]:
                f(eng)

        @block.tensor
        def _(eng):
            for f in prog.queue["pe"]:
                f(eng)

        @block.scalar
        def _(eng):
            for f in prog.queue["act"]:
                f(eng)

        @block.vector
        def _(eng):
            for f in prog.queue["dve"]:
                f(eng)

        @block.gpsimd
        def _(eng):
            for f in prog.queue["pool"]:
                f(eng)


def kernel(**inputs):
    import numpy as np
    import concourse.bacc as bacc
    from concourse.bass_utils import run_bass_kernel_spmd

    nc = bacc.Bacc("TRN2", target_bir_lowering=False, num_devices=1)
    arrays, aps = {}, {}
    for name, value in inputs.items():
        a = np.ascontiguousarray(value)
        arrays[f"in_{name}"] = a
        aps[name] = nc.dram_tensor(f"in_{name}", a.shape, mybir.dt.from_np(a.dtype), kind="ExternalInput").ap()
    shape = inputs["x"].shape
    out = nc.dram_tensor("out_x", shape, F32, kind="ExternalOutput").ap()
    build(nc, aps, out)
    r = run_bass_kernel_spmd(nc, [arrays], core_ids=[0])
    return r.results[0]["out_x"]
```

```python
from contextlib import ExitStack

import concourse.bass as bass
import concourse.mybir as mybir

F32 = mybir.dt.float32
F16 = mybir.dt.float16
BF16 = mybir.dt.bfloat16
ALU = mybir.AluOpType
ACT = mybir.ActivationFunctionType
AX = mybir.AxisListType

P = 128
SLOT = 32
FAR = 2.0 ** 100


class Program:

    TAIL = {"sp": 2000.0, "pe": 315.0, "act": 269.0, "dve": 242.0, "pool": 190.0}

    def __init__(self, nc, ctx):
        self.nc, self.ctx = nc, ctx
        self.queue = {"sp": [], "pe": [], "act": [], "dve": [], "pool": []}
        self.waited = {e: {} for e in self.queue}
        self.count, self.sems, self.marks = {}, {}, {}
        self.clock = {e: 0.0 for e in self.queue}
        self.busy = {e: 0.0 for e in self.queue}
        self.done = {}
        self.step_end = 0.0
        self.now = 0.0
        self.parts = []

    def sem(self, name):
        if name not in self.sems:
            self.sems[name] = self.ctx.enter_context(self.nc.semaphore(name))
            self.count[name] = 0
        return self.sems[name]

    def op(self, engine, emit, signal=None, by=1, ns=60.0, after=0.0):
        self.clock[engine] += ns
        self.busy[engine] += ns
        end = self.clock[engine] + self.TAIL[engine] + after
        self.step_end = max(self.step_end, end)
        if signal is None:
            self.queue[engine].append(emit)
            return None
        s = self.sem(signal)
        self.count[signal] += by
        self.done[signal, self.count[signal]] = end
        self.queue[engine].append(lambda e: emit(e).then_inc(s, by))
        return (signal, self.count[signal])

    def wait(self, engine, *marks):
        for mark in marks:
            name, value = mark
            self.clock[engine] = max(self.clock[engine], self.done[mark])
            if self.waited[engine].get(name, 0) >= value:
                continue
            self.waited[engine][name] = value
            s = self.sems[name]
            self.queue[engine].append(lambda e, s=s, v=value: e.wait_ge(s, v))


class Ring:

    def __init__(self, tiles, done):
        self.done = done
        self.tiles, self.free = tiles, [[] for _ in tiles]
        self.idle = list(range(len(tiles)))
        self.free_at = [0.0] * len(tiles)

    def ready(self):
        return bool(self.idle)

    def take(self):
        i = min(self.idle, key=lambda j: self.free_at[j])
        self.idle.remove(i)
        return i, self.tiles[i], self.free[i]

    def release(self, i, *marks):
        self.idle.append(i)
        self.free_at[i] = max([self.done[m] for m in marks], default=0.0)
        self.free[i] = list(marks)


def build(nc, A, out):
    B, L, C = A["x"].shape
    H = 16
    D = C // H
    TOP = 16
    SHIFT = 64
    HID = A["L0_xcond_w_m2"].shape[0]
    CC = C // P
    LT = L // P
    HC = HID // P
    G4 = P // SLOT
    NG = H // G4
    assert (CC, LT, NG, D) == (2, 2, 4, 16) and TOP == 16 and SHIFT * 2 == P
    QSCALE = float(D) ** -0.5

    with ExitStack() as ctx:
        prog = Program(nc, ctx)
        op, wait = prog.op, prog.wait

        def sb(name, shape, dt):
            return ctx.enter_context(nc.sbuf_tensor(name, shape, dt))

        def ring(name, n, shape, dt):
            return Ring([sb(f"{name}{i}", shape, dt) for i in range(n)], prog.done)

        def psum(name, n):
            return Ring([ctx.enter_context(nc.psum_tensor(f"{name}{i}", [P, 512], F32)) for i in range(n)], prog.done)

        bank_any = psum("bank_any", 6)
        bank_out = psum("bank_out", 2)

        ident32 = sb("ident32", [P, P], F32)
        ident16 = sb("ident16", [P, P], BF16)
        minus_half = sb("minus_half", [P, LT], F32)

        NB = {"ada": 18, "qkv": 6, "so": 2, "q": 2, "kv": 4, "co": 2, "m1": 16, "m2": 2,
              "bq": 2, "bkv": 4, "bp": 2, "ssq": 4, "sskv": 4}
        bias_src = {"ada": "L0_xcond_b_ada", "qkv": "L0_xcond_b_qkv", "so": "L0_xcond_b_so",
                    "q": "L0_xcond_b_q", "kv": "L0_xcond_b_kv", "co": "L0_xcond_b_co",
                    "m1": "L0_xcond_b_m1", "m2": "L0_xcond_b_m2", "bq": "L1_xcond_bq",
                    "bkv": "L1_xcond_bkv", "bp": "L1_xcond_bp", "ssq": "L1_xcond_bss_q",
                    "sskv": "L1_xcond_bss_kv"}
        bias_at, rows = {}, 0
        for name, n in NB.items():
            bias_at[name] = rows
            rows += n
        NBR = rows
        bias_col = sb("bias_col", [P, NBR], F32)
        q_bias = sb("q_bias", [P, 3 * CC], F32)
        half_bias = sb("half_bias", [P, HC], F32)

        W = {}
        for name, src, k, n, scale in (
            ("qkv", "L0_xcond_w_qkv", CC, 3 * C, 1.0), ("so", "L0_xcond_w_so", CC, C, 1.0),
            ("q", "L0_xcond_w_q", CC, C, QSCALE), ("kv", "L0_xcond_w_kv", CC, 2 * C, 1.0),
            ("co", "L0_xcond_w_co", CC, C, 1.0), ("m1", "L0_xcond_w_m1", CC, 2 * HID, 1.0),
            ("m2", "L0_xcond_w_m2", HC, C, 1.0), ("Wq", "L1_xcond_Wq", CC, C, QSCALE),
            ("Wkv", "L1_xcond_Wkv", CC, 2 * C, 1.0), ("Wp", "L1_xcond_Wp", CC, C, 1.0),
        ):
            W[name] = dict(src=A[src].rearrange("(k p) n -> p k n", p=P), k=k, n=n, scale=scale,
                           hi=sb(f"w_{name}_hi", [P, k, n], F16), lo=sb(f"w_{name}_lo", [P, k, n], F16))
        NA = NB["ada"]
        cond_T = sb("cond_T", [P, CC, B], F32)
        cond_t = sb("cond_t", [P, CC, B], F32)
        cond_s = sb("cond_s", [P, CC, B], F32)
        ada = sb("ada", [P, NA, B], F32)
        gate_bias = sb("gate_bias", [P, 3 * CC, B], F32)
        half_gate = sb("half_gate", [P, CC, B], F32)
        ssq = sb("ssq", [P, NB["ssq"], B], F32)
        sskv = sb("sskv", [P, NB["sskv"], B], F32)

        X_ring = ring("x_tile", 4, [P, LT, C], F32)
        ctx_ring = ring("ctx_tile", 2, [P, LT, C], F32)
        stats_ring = ring("stats", 4, [P, LT, 6], F32)
        mv_ring = ring("mean_var", 4, [P, LT, 2], F32)
        rstd_ring = ring("rstd", 4, [P, 3, LT], F32)
        norm_ring = ring("normed", 2, [P, LT, C], F32)
        full_ring = ring("full", 3, [P, CC, L], F32)
        pair_ring = ring("pair", 4, [P, 2, CC, L], F16)
        self_parts = ring("self_parts", 2, [P, 2, CC, L], F16)
        top_parts = ring("top_parts", 1, [P, 2, CC, L], F16)
        last_k_parts = ring("last_k_parts", 1, [P, 2, CC, L], F16)
        last_q_parts = ring("last_q_parts", 1, [P, 2, CC, L], F16)
        values = {kind: ring(f"v_{kind}", n, [P, LT, H, SLOT], F32) for kind, n in
                  (("soft", 3), ("top", 2))}
        tanh_ring = ring("tanh", 2, [P, 2, L], F32)
        gated_ring = ring("gated", 2, [P, 2, L], F32)
        hid_ring = ring("hid", 1, [P, 2, HC, L], F16)
        prob_ring = ring("prob", 5, [P, 512], F32)
        osum_ring = ring("osum", 3, [P, NG, L], F32)
        recip_ring = ring("recip", 4, [P, H], F32)
        rest_ring = ring("rest", 4, [P, L], F32)
        best_ring = ring("best", 4, [P, LT, 8], F32)
        far_ring = ring("far", 10, [P, LT, L], BF16)
        rowmax_ring = ring("rowmax", 3, [P, 8, LT, 8], F32)
        guard_ring = ring("guard", 3, [16, P], F16)

        NR = 3 * D
        PARTS = {"q": (0, 1, 0), "k": (0, 0, 1)}
        stacks, slots = {}, []
        for pair_of in (("top0", "top1"), ("soft0", "soft1")):
            halves = {w: sb(f"{w}_stack_{pair_of[0]}_{pair_of[1]}", [P, H, L], F16) for w in "qk"}
            for name, base in zip(pair_of, (0, P // 2)):
                slots.append(dict(
                    name=name, tile=halves, base=base,
                    q=halves["q"][base:base + NR + 1, :, :], k=halves["k"][base:base + NR + 1, :, :],
                    dq=nc.dram_tensor(f"dq_{name}", (2, C, L), F16, kind="Internal").ap(),
                    dk=nc.dram_tensor(f"dk_{name}", (2, C, L), F16, kind="Internal").ap(),
                    dm=nc.dram_tensor(f"dm_{name}", (H, LT, P), F16, kind="Internal").ap()))
        for kind in ("top", "soft"):
            stacks[kind] = Ring([s for s in slots if s["name"][:-1] == kind], prog.done)
        stage_cols = 4 * C
        stage = [sb(f"stage{i}", [P, stage_cols], F32) for i in range(2)]
        cond = stage[1][0:B, 0:C]
        bias_rows = stage[1][0:NBR, C:C + P]

        def cols(o):
            return o.free_size()

        def mm(o, lhsT, rhs, start, stop, signal=None):
            n = cols(rhs)
            ns = (0.43 if lhsT.dtype == F16 and n == L else 0.7) * n
            return op("pe", lambda e: e.matmul(o, lhsT, rhs, start=start, stop=stop), signal,
                      ns=128.0 * n / L if n >= P and lhsT.free_size() == SLOT else max(27.0, ns))

        def turn(o, i, signal=None):
            n = i.partition_size()
            return op("pe", lambda e: e.transpose(o, i, ident32[0:n, 0:n]), signal, ns=109.0 * n / P)

        def act(o, i, f, signal=None, **kw):
            return op("act", lambda e: e.activation(o, i, f, **kw), signal,
                      ns=51 + cols(i) / 1.2 + 93 * sum(not isinstance(v, float) for v in kw.values()))

        def dma(o, i, signal):
            return op("sp", lambda e: e.dma_start(o, i), signal, 16, ns=60.0, after=600.0)

        def dve(o, emit, signal=None, n=None):
            return op("dve", emit, signal, ns=((n or cols(o)) + 66) / 0.96)

        def dve_tt(o, a, b, f, signal=None):
            return dve(o, lambda e: e.tensor_tensor(o, a, b, f), signal)

        def dve_ts(o, a, s1, s2, f0, f1, signal=None):
            return dve(o, lambda e: e.tensor_scalar(o, a, s1, s2, f0, f1), signal)

        def dve_stt(o, a, s, b, f0, f1, signal=None):
            return dve(o, lambda e: e.scalar_tensor_tensor(o, a, s, b, f0, f1), signal, cols(o) + 58)

        def dve_max8(o, i, signal):
            return dve(o, lambda e: e.max(o, i), signal, cols(i))

        def dve_replace(o, what, i, signal):
            return dve(o, lambda e: e.match_replace(o, what, i, -FAR), signal)

        def dve_rowmax(o, i, signal):
            return dve(o, lambda e: e.tensor_reduce(o, i, AX.X, ALU.max), signal, cols(i))

        def dve_reciprocal(o, i, signal):
            return dve(o, lambda e: e.reciprocal(o, i), signal, 90)

        def pool_tt(o, a, b, f, signal=None):
            per = 165.0 if f == ALU.pow else 1.95
            return op("pool", lambda e: e.tensor_tensor(o, a, b, f), signal, ns=150 + per * cols(o))

        def pool_ts(o, a, s1, s2, f0, f1, signal=None):
            return op("pool", lambda e: e.tensor_scalar(o, a, s1, s2, f0, f1), signal,
                      ns=(300 if cols(o) == L else 160) + cols(o) / 1.2)

        def prologue():
            marks = prog.marks
            z = op("pool", lambda e: e.memset(ident32[:, :], 0.0), "const")
            z = op("pool", lambda e: e.memset(ident16[:, :], 0.0), "const")
            wait("pool", z)
            for t in (ident32, ident16):
                one = op("pool", lambda e, t=t: e.affine_select(
                    out=t[:, :], in_=t[:, :], compare_op=ALU.not_equal, fill=1.0, base=0,
                    pattern=[[-1, P]], channel_multiplier=1), "const")
            marks["const"] = one
            op("dve", lambda e: e.memset(minus_half[:, :], -0.5), "filled")
            for kind in stacks:
                for s in stacks[kind].tiles:
                    lo = s["base"] + SLOT
                    op("dve", lambda e, s=s, lo=lo: e.memset(s["tile"]["k"][lo:lo + SLOT, :, :], 1.0), "filled")
            for v in [v for r in values.values() for v in r.tiles]:
                marks["ones_filled"] = op("dve", lambda e, v=v: e.memset(v[:, :, :, D:SLOT], 1.0), "filled")
            for name, src in bias_src.items():
                at = bias_at[name]
                m = dma(bias_rows[at:at + NB[name], :], A[src].rearrange("(m p) -> m p", p=P), "small_in")
            m = dma(cond, A["cond_1024"], "small_in")
            wait("pe", marks["const"], m)
            i, bank, _ = bank_any.take()
            turn(bank[:, 0:NBR], bias_rows)
            for c in range(CC):
                t = turn(bank[:, 128 + B * c:128 + B * (c + 1)], cond[:, c * P:(c + 1) * P], "pe_pre")
            marks["cond_read"] = t
            wait("act", t)
            act(bias_col[:, :], bank[:, 0:NBR], ACT.Copy)
            cT = bank[:, 128:128 + CC * B].rearrange("p (c b) -> p c b", c=CC)
            act(cond_T[:, :, :], cT, ACT.Copy)
            t = act(cond_t[:, :, :], cT, ACT.Tanh, "act_pre", scale=0.5)
            bank_any.release(i, t)
            wait("dve", t, m)
            t = dve_stt(cond_s[:, :, :], cond_t[:, :, :], 1.0, cond_T[:, :, :], ALU.add, ALU.mult, "dve_pre")
            wait("dve", t)
            t = dve_ts(cond_T[:, :, :], cond_s[:, :, :], 0.5, None, ALU.mult, ALU.bypass, "dve_pre")
            marks["cond"] = t
            for j, name in enumerate(("qkv", "q", "bq")):
                dve_ts(q_bias[:, CC * j:CC * (j + 1)], bias_col[:, bias_at[name]:bias_at[name] + CC],
                       QSCALE, None, ALU.mult, ALU.bypass)
            marks["bias"] = dve_ts(half_bias[:, :], bias_col[:, bias_at["m1"]:bias_at["m1"] + HC], 0.5, None,
                                   ALU.mult, ALU.bypass, "dve_pre")
            yield
            stage_free = [[], [marks["cond_read"]]]
            turn_no = [0]

            def staged(src, k, n):
                i = turn_no[0] % 2
                turn_no[0] += 1
                wait("sp", *stage_free[i])
                view = stage[i][:, 0:k * n].rearrange("p (k n) -> p k n", k=k)
                return i, view, dma(view, src, f"stage_in{i}")

            def modulation(dst, src, bias, m0, n):
                si, view, landed = staged(
                    A[src].rearrange("(k p) n -> p k n", p=P)[:, :, m0 * P:(m0 + n) * P], CC, n * P)
                i, bank, free = bank_any.take()
                wait("pe", landed, marks["cond"], *free)
                for m in range(n):
                    for c in range(CC):
                        t = mm(bank[:, m * B:(m + 1) * B], view[:, c, m * P:(m + 1) * P], cond_T[:, c, :],
                               c == 0, c == CC - 1, "pe_pre" if (m, c) == (n - 1, CC - 1) else None)
                stage_free[si] = [t]
                at = bias_at[bias] + m0
                wait("dve", t)
                t = dve_tt(dst[:, m0:m0 + n, :], bank[:, 0:n * B].rearrange("p (m b) -> p m b", b=B),
                           bias_col[:, at:at + n].unsqueeze(2).broadcast_to([P, n, B]), ALU.add, "dve_pre")
                bank_any.release(i, t)
                wait("dve", t)
                return t

            def plus_one(scale):
                return dve_ts(scale, scale, 1.0, None, ALU.add, ALU.bypass, "dve_pre")

            def gate(j, name):
                g, at = 2 * (3 * j + 2), bias_at[name]
                return dve_tt(gate_bias[:, CC * j:CC * (j + 1), :], ada[:, g:g + 2, :],
                              bias_col[:, at:at + 2].unsqueeze(2).broadcast_to([P, CC, B]), ALU.mult, "dve_pre")

            def weights(name):
                w = W[name]
                width = min(w["n"], stage_cols // w["k"] // P * P)
                for n0 in range(0, w["n"], width):
                    n = min(width, w["n"] - n0)
                    si, view, landed = staged(w["src"][:, :, n0:n0 + n], w["k"], n)
                    hi, lo = w["hi"][:, :, n0:n0 + n], w["lo"][:, :, n0:n0 + n]
                    parts = [(0, n, w["scale"])]
                    if name == "qkv":
                        parts = [(max(0, a - n0), min(n, b - n0), s) for a, b, s in
                                 ((0, C, QSCALE), (C, 3 * C, 1.0)) if max(n0, a) < min(n0 + n, b)]
                    wait("act", landed)
                    for a, b, s in parts:
                        t = act(hi[:, :, a:b], view[:, :, a:b], ACT.Copy, "act_pre", scale=s)
                    wait("dve", t)
                    for a, b, s in parts:
                        t = dve_stt(lo[:, :, a:b], view[:, :, a:b], s, hi[:, :, a:b], ALU.mult, ALU.subtract,
                                    "dve_pre")
                    stage_free[si] = [t]
                w["mark"] = t

            modulation(ada, "L0_xcond_w_ada", "ada", 0, 4)
            marks["ada_self"] = plus_one(ada[:, 2:4, :])
            yield
            weights("qkv")
            yield
            modulation(ada, "L0_xcond_w_ada", "ada", 4, 4)
            modulation(ada, "L0_xcond_w_ada", "ada", 8, 4)
            plus_one(ada[:, 8:10, :])
            marks["ada_top"] = gate(0, "so")
            yield
            for name in ("so", "q", "kv"):
                weights(name)
                yield
            modulation(ada, "L0_xcond_w_ada", "ada", 12, 4)
            modulation(ada, "L0_xcond_w_ada", "ada", 16, 2)
            plus_one(ada[:, 14:16, :])
            dve_ts(half_gate[:, :, :], ada[:, 16:18, :], 0.5, None, ALU.mult, ALU.bypass, "dve_pre")
            gate(1, "co")
            marks["ada_mlp"] = gate(2, "m2")
            yield
            for name in ("co", "m1", "m2"):
                weights(name)
                yield
            for dst, src, bias in ((sskv, "L1_xcond_Wss_kv", "sskv"), (ssq, "L1_xcond_Wss_q", "ssq")):
                modulation(dst, src, bias, 0, 4)
                marks["ada_last"] = plus_one(dst[:, 0:2, :])
            for name in ("Wkv", "Wq", "Wp"):
                weights(name)
                yield
            for i in range(2):
                for j in range(0, stage_cols, LT * C):
                    X_ring.tiles.append(stage[i][:, j:j + LT * C].rearrange("p (t c) -> p t c", t=LT))
                    X_ring.free.append(None)
                    X_ring.free_at.append(0.0)
                    X_ring.release(len(X_ring.tiles) - 1, *stage_free[i])

        def held(*rings):
            while not all(r.ready() for r in rings):
                yield
            at = max(min(r.free_at[i] for i in r.idle) for r in rings)
            if at > prog.now:
                prog.step_end = max(prog.step_end, at)
                yield
                yield from held(*rings)

        def due(*marks):
            at = max(prog.done[m] for m in marks)
            if at > prog.now:
                prog.step_end = max(prog.step_end, at)
                yield

        def together(*steps):
            left = [len(steps)]

            def run(g):
                yield from g
                left[0] -= 1

            for g in steps:
                prog.parts.append([prog.now, run(g), False])
            while left[0]:
                yield

        def modulated(name):
            while name not in prog.marks:
                yield
            yield from due(prog.marks[name])
            wait("act", prog.marks[name], prog.marks["bias"])

        def weights_ready(w):
            while "mark" not in w:
                yield

        def layer_norm(src, src_marks, scale, shift, eps, result):
            yield from due(*src_marks)
            yield from held(stats_ring, mv_ring, rstd_ring, norm_ring)
            si, stats, sfree = stats_ring.take()
            mi, mv, mfree = mv_ring.take()
            ri, rstd, rfree = rstd_ring.take()
            ni, norm, nfree = norm_ring.take()
            wait("dve", *src_marks, *sfree, *mfree)
            for t in range(LT):
                m = dve(None, lambda e, t=t: e.bn_stats(stats[:, t, :], src[:, t, :]), "dve_ln", C)
            yield
            wait("dve", m)
            for t in range(LT):
                m = dve(None, lambda e, t=t: e.bn_aggr(mv[:, t, :], stats[:, t, :]), "dve_ln", 26)
            stats_ring.release(si, m)
            yield
            wait("pool", m, prog.marks["ones_filled"], *rfree, *nfree)
            m = pool_ts(rstd[:, 0, :], mv[:, :, 1], eps, 1.0, ALU.add, ALU.mult, "pool_ln")
            wait("pool", m)
            m = pool_tt(rstd[:, 1, :], rstd[:, 0, :], minus_half[:, :], ALU.pow, "pool_ln")
            wait("pool", m)
            m = pool_tt(rstd[:, 0, :], mv[:, :, 0], rstd[:, 1, :], ALU.mult, "pool_ln")
            wait("pool", m)
            m = pool_ts(rstd[:, 2, :], rstd[:, 0, :], -1.0, 0.0, ALU.mult, ALU.add, "pool_ln")
            mv_ring.release(mi, m)
            wait("pool", m)
            for t in range(LT):
                m = pool_ts(norm[:, t, :], src[:, t, :], rstd[:, 1, t:t + 1], rstd[:, 2, t:t + 1],
                            ALU.mult, ALU.add, "pool_ln")
            rstd_ring.release(ri, m)
            result["read"] = m
            yield
            yield
            yield from bank_to_split(result)
            bi, bank, bfree = bank_any.take()
            wait("pe", m, *bfree)
            for c in range(CC):
                for t in range(LT):
                    m = turn(bank[:, c * L + t * P:c * L + (t + 1) * P], norm[:, t, c * P:(c + 1) * P],
                             "pe_turn" if (c, t) == (CC - 1, LT - 1) else None)
            norm_ring.release(ni, m)
            yield from split(bi, bank, m, [(scale(c), shift(c)) for c in range(CC)], result)

        def bank_to_split(result, pairs=pair_ring):
            yield from held(bank_any, full_ring, pairs)
            result["full"], result["taken"], result["ring"] = full_ring.take(), pairs.take(), pairs

        def split(bi, bank, mark, affine, result):
            fi, full, ffree = result["full"]
            pi, pair, pfree = result["taken"]
            yield
            wait("act", mark, *ffree)
            view = bank[:, :].rearrange("p (c l) -> p c l", c=CC)
            if affine is None:
                m = act(full[:, :, :], view, ACT.Copy, "act_full")
            else:
                for c, (s, b) in enumerate(affine):
                    kw = dict(bias=b) if s is None else dict(scale=s, bias=b)
                    m = act(full[:, c, :], view[:, c, :], ACT.Identity, "act_full", **kw)
            bank_any.release(bi, m)
            wait("act", m, *pfree)
            m = act(pair[:, 0, :, :], full[:, :, :], ACT.Copy, "act_split")
            yield
            wait("pool", m)
            m2 = pool_tt(pair[:, 1, :, :], full[:, :, :], pair[:, 0, :, :], ALU.subtract, "pool_split")
            full_ring.release(fi, m2)
            result.update(pair=pair, index=pi, marks=[m, m2])
            yield

        def project(bank_at, w, cols, pair, chunks, signal):
            for k in range(chunks):
                for n, (a, b) in enumerate((("hi", 0), ("hi", 1), ("lo", 0))):
                    last = k == chunks - 1 and n == 2
                    m = mm(bank_at, w[a][:, k, cols], pair[:, b, k, :], k == 0 and n == 0, last,
                           signal if last else None)
            return m

        def to_stack(slot, which, res):
            s, name, d = slot[which], slot["name"] + which, slot["d" + which]
            wait("sp", prog.marks["ones_filled"], *res["marks"], *slot.get("scratch_free_" + which, []))
            for part in range(2):
                m = dma(d[part].rearrange("(c p) l -> p c l", p=P), res["pair"][:, part, :, :], f"to_{name}")
            res["ring"].release(res["index"], m)
            wait("sp", m, *slot.get("free", []))
            for r, part in enumerate(PARTS[which]):
                m = dma(s[r * D:(r + 1) * D, :, :], d[part].rearrange("(h d) l -> d h l", d=D), f"from_{name}")
            slot["scratch_free_" + which] = [m]
            slot[which + "_mark"] = m

        def project_values(w, col0, h, ring, v):
            yield from weights_ready(w)
            yield from held(bank_any, ring)
            bi, bank, bfree = bank_any.take()
            v["ring"] = ring
            v["index"], v["tile"], vfree = ring.take()
            pair = h["pair"]
            wait("pe", *h["marks"], w["mark"], prog.marks["ones_filled"], *bfree)
            for t in range(LT):
                o = bank[:, t * C:(t + 1) * C]
                for k in range(CC):
                    for n, (a, b) in enumerate(((0, "hi"), (1, "hi"), (0, "lo"))):
                        last = k == CC - 1 and n == 2
                        m = mm(o, pair[:, a, k, t * P:(t + 1) * P], w[b][:, k, col0:col0 + C],
                               k == 0 and n == 0, last,
                               "pe_v" if last and t == LT - 1 else None)
            h["reads"] = h.get("reads", []) + [m]
            yield
            wait("act", m, *vfree)
            v["mark"] = act(v["tile"][:, :, :, 0:D].rearrange("p t h d -> p (t h) d"),
                            bank[:, :].rearrange("p (g d) -> p g d", d=D), ACT.Copy, "act_v")
            bank_any.release(bi, v["mark"])

        def project_parts(w, col0, bias, h, pairs, res):
            yield from weights_ready(w)
            yield from bank_to_split(res, pairs)
            bi, bank, bfree = bank_any.take()
            wait("pe", *h["marks"], w["mark"], *bfree)
            for c in range(CC):
                m = project(bank[:, c * L:(c + 1) * L], w, slice(col0 + c * P, col0 + (c + 1) * P), h["pair"], CC,
                            "pe_qk")
            h["reads"] = h.get("reads", []) + [m]
            yield from split(bi, bank, m, [(None, bias(c)) for c in range(CC)], res)

        def query_bias(j):
            return lambda c: q_bias[:, CC * j + c:CC * j + c + 1]

        def bias_at_chunk(at):
            return lambda c: bias_col[:, at + c:at + c + 1]

        def guard(slot, rm, h0, n, mark, done):
            yield from held(bank_any, guard_ring)
            bi, bank, bfree = bank_any.take()
            gi, g, gfree = guard_ring.take()
            wait("pe", mark, *bfree)
            m = turn(bank[0:n * LT, 0:P], rm[:, 0:n, :, 0].rearrange("p h t -> p (h t)"), "pe_turn")
            yield
            wait("act", m, *gfree)
            m = act(g[0:n * LT, :], bank[0:n * LT, 0:P], ACT.Copy, "act_guard", scale=-1.0)
            bank_any.release(bi, m)
            name = slot["name"]
            wait("sp", m, *slot.get(("scratch_free_m", h0), []))
            m = dma(slot["dm"][h0:h0 + n].rearrange("h t l -> (h t) l"), g[0:n * LT, :], f"to_m{name}_{h0}")
            guard_ring.release(gi, m)
            wait("sp", m, *slot.get("free", []))
            m = dma(slot["q"][NR:NR + 1, h0:h0 + n, :],
                    slot["dm"][h0:h0 + n].rearrange("(o h) t l -> o h (t l)", o=1), f"from_m{name}_{h0}")
            slot["scratch_free_m", h0] = [m]
            done["mark"] = m
            yield

        def attend_group(slot, osum, g, window, far, marks):
            q, k, v = slot["q"], slot["k"], slot["v"]["tile"]
            step = 2 if window else 1
            todo = []
            yield from held(bank_out)
            out_bank = bank_out.take()
            for h0 in range(g * G4, (g + 1) * G4, step):
                yield from held(bank_any, prob_ring)
                bi, bank, bfree = bank_any.take()
                pi, prob, pfree = prob_ring.take()
                wait("pe", slot["v"]["mark"], slot["q_mark"], slot["k_mark"], prog.marks["ones_filled"], *marks, *bfree)
                for h in range(h0, h0 + step):
                    for t in range(LT):
                        if window:
                            at = ((h - h0) * LT + t) * P
                            m = mm(bank[:, at:at + P], k[:, h, t * P:(t + 1) * P], q[:, h, t * P:(t + 1) * P],
                                   True, True, "pe_prob")
                            continue
                        o = bank[:, t * L:(t + 1) * L]
                        m = mm(o, k[:, h, t * P:(t + 1) * P], q[:, h, :], True, far is None,
                               "pe_prob" if far is None else None)
                        if far is not None:
                            fi, ftile, fmark = far[h % G4]
                            wait("pe", fmark)
                            for j in range(LT):
                                m = mm(o[:, j * P:(j + 1) * P], ftile[:, j, t * P:(t + 1) * P], ident16[:, :],
                                       False, j == LT - 1, "pe_prob" if j == LT - 1 else None)
                if far is not None:
                    far_ring.release(far[h0 % G4][0], m)
                wait("act", m, *pfree)
                e = act(prob[:, :], bank[:, :], ACT.Exp, "act_exp")
                bank_any.release(bi, e)
                todo.append((h0, pi, prob, e))
                yield
                if len(todo) == 2:
                    values_of(*todo.pop(0), window, step, g, out_bank, v)
            while todo:
                m = values_of(*todo.pop(0), window, step, g, out_bank, v)
                if todo:
                    yield
            oi, obank, _ = out_bank
            wait("act", m, *osum["free"])
            osum["mark"] = act(osum["tile"][:, g, :], obank[:, 0:L], ACT.Copy, "act_osum")
            bank_out.release(oi, osum["mark"])
            return m

        def values_of(h0, pi, prob, e, window, step, g, out_bank, v):
            _, obank, ofree = out_bank
            wait("pe", e, *ofree)
            for h in range(h0, h0 + step):
                j = (h - g * G4) * SLOT
                for t in range(LT):
                    if window:
                        m = mm(obank[j:j + SLOT, t * P:(t + 1) * P], v[:, t, h, :],
                               prob[:, ((h - h0) * LT + t) * P:((h - h0) * LT + t + 1) * P], True, True, "pe_pv")
                    else:
                        m = mm(obank[j:j + SLOT, 0:L], v[:, t, h, :], prob[:, t * L:(t + 1) * L],
                               t == 0, t == LT - 1, "pe_pv")
            prob_ring.release(pi, m)
            return m

        def row_maxima(slot, window, h8, done):
            q, k = slot["q"], slot["k"]
            yield from due(slot["q_mark"], slot["k_mark"])
            yield from held(rowmax_ring)
            ri, rm, rfree = rowmax_ring.take()
            step = 2 if window else 1
            for h0 in range(h8, h8 + 8, step):
                yield from held(bank_any)
                bi, bank, bfree = bank_any.take()
                wait("pe", slot["q_mark"], slot["k_mark"], *bfree)
                for h in range(h0, h0 + step):
                    for t in range(LT):
                        if window:
                            at = ((h - h0) * LT + t) * P
                            m = mm(bank[:, at:at + P], q[0:NR, h, t * P:(t + 1) * P],
                                   k[0:NR, h, t * P:(t + 1) * P], True, True, "pe_score")
                        else:
                            m = mm(bank[:, t * L:(t + 1) * L], q[0:NR, h, t * P:(t + 1) * P], k[0:NR, h, :],
                                   True, True, "pe_score")
                yield from due(m)
                wait("dve", m, *rfree)
                m = dve_rowmax(rm[:, h0 - h8:h0 - h8 + step, :, 0],
                               bank[:, :].rearrange("p (h t k) -> p h t k", h=step, t=LT), "dve_max")
                bank_any.release(bi, m)
            d = {}
            yield
            yield from guard(slot, rm, h8, 8, m, d)
            rowmax_ring.release(ri, d["mark"])
            done[h8] = d["mark"]

        def attend(slot, window, osum):
            done = {}
            yield from together(*[row_maxima(slot, window, h8, done) for h8 in range(0, H, 8)])
            for g in range(NG):
                yield from due(done[g * G4 // 8 * 8])
                m = yield from attend_group(slot, osum, g, window, None, [done[g * G4 // 8 * 8]])
                yield
            slot["free"] = [m]
            slot["v"]["ring"].release(slot["v"]["index"], m)

        def finish_attention(osum, value_bias, w, scale, shift, X, result):
            yield from weights_ready(w)
            yield from due(osum["mark"])
            yield from held(norm_ring)
            ni, norm, nfree = norm_ring.take()
            for t in range(LT):
                yield from held(bank_any, recip_ring)
                bi, bank, bfree = bank_any.take()
                ri, rc, rfree = recip_ring.take()
                wait("pe", osum["mark"], *bfree)
                for g in range(NG):
                    m = turn(bank[:, g * P:(g + 1) * P], osum["tile"][:, g, t * P:(t + 1) * P],
                             "pe_turn" if g == NG - 1 else None)
                yield
                heads = bank[:, :].rearrange("p (h s) -> p h s", s=SLOT)
                wait("dve", m, *rfree, *nfree)
                m2 = dve_reciprocal(rc[:, :], heads[:, :, D], "dve_norm")
                yield
                wait("dve", m2)
                m2 = dve_tt(norm[:, t, :].rearrange("p (h d) -> p h d", d=D), heads[:, :, 0:D],
                            rc[:, :].unsqueeze(2).broadcast_to([P, H, D]), ALU.mult, "dve_norm")
                bank_any.release(bi, m2)
                recip_ring.release(ri, m2)
            osum_ring.release(osum["index"], m)
            yield
            res = {}
            yield from bank_to_split(res)
            bi, bank, bfree = bank_any.take()
            wait("pe", m2, *bfree)
            for c in range(CC):
                for t in range(LT):
                    m = turn(bank[:, c * L + t * P:c * L + (t + 1) * P], norm[:, t, c * P:(c + 1) * P],
                             "pe_turn" if (c, t) == (CC - 1, LT - 1) else None)
            norm_ring.release(ni, m)
            yield from split(bi, bank, m, [(None, value_bias(c)) for c in range(CC)], res)
            yield from held(bank_any)
            bi, bank, bfree = bank_any.take()
            wait("pe", *res["marks"], w["mark"], *bfree)
            for c in range(CC):
                m = project(bank[:, c * L:(c + 1) * L], w, slice(c * P, (c + 1) * P), res["pair"], CC, "pe_out")
            pair_ring.release(res["index"], m)
            yield
            yield from add_rows(bi, bank, m, scale, shift, X, result)

        def add_rows(bi, bank, mark, scale, shift, X, result):
            yield from held(full_ring)
            fi, full, ffree = full_ring.take()
            wait("act", mark, *ffree)
            for c in range(CC):
                kw = dict(bias=shift(c)) if scale is None else dict(scale=scale(c), bias=shift(c))
                m = act(full[:, c, :], bank[:, c * L:(c + 1) * L], ACT.Identity, "act_out", **kw)
            bank_any.release(bi, m)
            yield
            yield from held(bank_any)
            bi, bank, bfree = bank_any.take()
            wait("pe", m, *bfree)
            for t in range(LT):
                for c in range(CC):
                    m = turn(bank[:, t * C + c * P:t * C + (c + 1) * P], full[:, c, t * P:(t + 1) * P],
                             "pe_turn" if (c, t) == (CC - 1, LT - 1) else None)
            full_ring.release(fi, m)
            yield
            wait("dve", m, *result["marks"])
            m = dve_tt(X[:, :, :], X[:, :, :], bank[:, :].rearrange("p (t c) -> p t c", t=LT), ALU.add, "dve_x")
            bank_any.release(bi, m)
            result["marks"] = [m]
            yield

        projected, attended, x_of, top_keys, top_slot, top_osum, mlp_in = {}, {}, {}, {}, {}, {}, {}
        mlp_done, last_keys, last_query, last_osum = {}, {}, {}, {}
        top_scores, top_maxima, top_groups = [], [], []

        def roll_copy(b, tile, load, signal):
            dram = A["x"] if load else out
            for rows, at in ((slice(SHIFT, SHIFT + P), tile[:, 0, :]),
                             (slice(SHIFT + P, L), tile[0:L - SHIFT - P, 1, :]),
                             (slice(0, SHIFT), tile[L - SHIFT - P:P, 1, :])):
                m = dma(at, dram[b, rows, :], signal) if load else dma(dram[b, rows, :], at, signal)
            return m

        def ada_at(i, b, src=ada):
            return lambda c: src[:, 2 * i + c, b:b + 1]

        def load_part():
            for b in range(B):
                yield from held(X_ring)
                xi, X, xfree = X_ring.take()
                wait("sp", *xfree)
                m = roll_copy(b, X, True, f"x_in{xi}")
                x_of[b] = dict(index=xi, tile=X, marks=[m])
                yield
                while b - 1 not in projected and b > 0:
                    yield

        def self_part():
            yield from modulated("ada_self")
            for b in range(B):
                while b not in x_of:
                    yield
                xs = x_of[b]
                h = {}
                yield from layer_norm(xs["tile"], xs["marks"], ada_at(1, b), ada_at(0, b), 1e-6, h)
                w = W["qkv"]
                p = dict(q={}, k={}, v={})
                yield from together(
                    project_parts(w, 0, query_bias(0), h, self_parts, p["q"]),
                    project_parts(w, C, bias_at_chunk(bias_at["qkv"] + CC), h, self_parts, p["k"]),
                    project_values(w, 2 * C, h, values["soft"], p["v"]))
                pair_ring.release(h["index"], *h["reads"])
                projected[b] = p
                yield

        def window_part(first):
            for b in range(first, B, 2):
                while b not in projected:
                    yield
                yield from held(stacks["soft"])
                ki, slot, _ = stacks["soft"].take()
                p = projected[b]
                for which in "qk":
                    to_stack(slot, which, p[which])
                slot["v"] = p["v"]
                yield
                yield from held(osum_ring)
                oi, ot, ofree = osum_ring.take()
                osum = dict(index=oi, tile=ot, free=ofree)
                yield from attend(slot, True, osum)
                stacks["soft"].release(ki)
                attended[b] = osum
                yield

        def query_part():
            yield from modulated("ada_top")
            for b in range(B):
                while b not in attended:
                    yield
                xs = x_of[b]
                X = xs["tile"]
                yield from finish_attention(attended[b], bias_at_chunk(bias_at["qkv"] + 2 * CC), W["so"], ada_at(2, b),
                                            lambda c, b=b: gate_bias[:, c, b:b + 1], X, xs)
                h = {}
                yield from layer_norm(X, xs["marks"], ada_at(4, b), ada_at(3, b), 1e-6, h)
                while b not in top_keys:
                    yield
                slot = top_keys[b]
                q = {}
                yield from project_parts(W["q"], 0, query_bias(1), h, top_parts, q)
                pair_ring.release(h["index"], *h["reads"])
                to_stack(slot, "q", q)
                top_slot[b] = slot
                yield

        def load_context(b, cm):
            ci, ct, cfree = ctx_ring.take()
            wait("sp", *cfree)
            cm["mark"] = dma(ct[:, :, :], A["ctx_1024"][b].rearrange("(t p) c -> p t c", p=P), f"ctx_in{ci}")
            cm["index"], cm["tile"] = ci, ct

        def top_keys_part():
            while "bias" not in prog.marks:
                yield
            wait("act", prog.marks["bias"])
            for b in range(B):
                yield from held(stacks["top"], ctx_ring)
                ki, slot, _ = stacks["top"].take()
                cm = {}
                load_context(b, cm)
                yield
                h, k, v = {}, {}, {}
                yield from bank_to_split(h)
                bi, bank, bfree = bank_any.take()
                wait("pe", cm["mark"], *bfree)
                for c in range(CC):
                    for t in range(LT):
                        m = turn(bank[:, c * L + t * P:c * L + (t + 1) * P], cm["tile"][:, t, c * P:(c + 1) * P],
                                 "pe_turn" if (c, t) == (CC - 1, LT - 1) else None)
                ctx_ring.release(cm["index"], m)
                yield from split(bi, bank, m, None, h)
                yield from together(
                    project_parts(W["kv"], 0, bias_at_chunk(bias_at["kv"]), h, top_parts, k),
                    project_values(W["kv"], C, h, values["top"], v))
                pair_ring.release(h["index"], *h["reads"])
                to_stack(slot, "k", k)
                slot["ring_index"], slot["v"] = ki, v
                top_keys[b] = slot
                yield

        def top_scores_part():
            for b in range(B):
                while b not in top_slot:
                    yield
                slot = top_slot[b]
                yield from due(slot["q_mark"], slot["k_mark"])
                q, k = slot["q"], slot["k"]
                for h in range(H):
                    while len(top_scores) > 1:
                        yield
                    yield from held(bank_any)
                    bi, bank, bfree = bank_any.take()
                    wait("pe", slot["q_mark"], slot["k_mark"], *bfree)
                    for t in range(LT):
                        m = mm(bank[:, t * L:(t + 1) * L], q[0:NR, h, t * P:(t + 1) * P], k[0:NR, h, :],
                               True, True, "pe_top")
                    top_scores.append((bi, bank, m))
                    yield

        def top_part():
            for b in range(B):
                for g in range(NG):
                    yield from held(rowmax_ring)
                    ri, rm, rfree = rowmax_ring.take()
                    far = []
                    for hj in range(G4):
                        yield from held(best_ring, far_ring)
                        while not top_scores:
                            yield
                        yield from due(top_scores[0][2])
                        bi, bank, m = top_scores.pop(0)
                        e8, best, efree = best_ring.take()
                        fi, ftile, ffree = far_ring.take()
                        rests = []
                        for t in range(LT):
                            yield from held(rest_ring)
                            rests.append(rest_ring.take())
                        wait("dve", m, *rfree, *efree, *ffree)
                        top8 = [dve_max8(rm[:, hj, t, :], bank[:, t * L:(t + 1) * L], "dve_top")
                                for t in range(LT)]
                        yield
                        part = []
                        for t in range(LT):
                            wait("dve", top8[t], *rests[t][2])
                            part.append(dve_replace(rests[t][1][:, :], rm[:, hj, t, :],
                                                    bank[:, t * L:(t + 1) * L], "dve_top"))
                        bank_any.release(bi, part[-1])
                        yield
                        for t in range(LT):
                            wait("dve", part[t])
                            top8[t] = dve_max8(best[:, t, :], rests[t][1][:, :], "dve_top")
                        yield
                        for t in range(LT):
                            wait("dve", top8[t])
                            m = dve_replace(ftile[:, t, :], best[:, t, :], rests[t][1][:, :], "dve_top")
                            rest_ring.release(rests[t][0], m)
                        best_ring.release(e8, m)
                        wait("pool", m)
                        m2 = pool_ts(ftile[:, :, :], ftile[:, :, :], FAR, -1.0, ALU.add, ALU.mult, "pool_far")
                        far.append((fi, ftile, m2))
                        yield
                    top_maxima.append((b, g, ri, rm, m, far))

        def top_guard_part():
            for _ in range(B * NG):
                while not top_maxima:
                    yield
                b, g, ri, rm, m, far = top_maxima.pop(0)
                yield from due(m)
                done = {}
                yield from guard(top_slot[b], rm, g * G4, G4, m, done)
                rowmax_ring.release(ri, done["mark"])
                top_groups.append((b, g, far, done["mark"]))

        def top_values_part():
            for _ in range(B * NG):
                while not top_groups:
                    yield
                b, g, far, mark = top_groups.pop(0)
                yield from due(mark)
                slot = top_slot[b]
                if g == 0:
                    yield from held(osum_ring)
                    oi, ot, ofree = osum_ring.take()
                    osum = dict(index=oi, tile=ot, free=ofree)
                m = yield from attend_group(slot, osum, g, False, far, [mark])
                if g == NG - 1:
                    slot["free"] = [m]
                    slot["v"]["ring"].release(slot["v"]["index"], m)
                    stacks["top"].release(slot["ring_index"])
                    top_osum[b] = osum
                yield

        def top_finish_part():
            yield from modulated("ada_mlp")
            for b in range(B):
                while b not in top_osum:
                    yield
                xs = x_of[b]
                X = xs["tile"]
                yield from finish_attention(top_osum[b], bias_at_chunk(bias_at["kv"] + CC), W["co"], ada_at(5, b),
                                            lambda c, b=b: gate_bias[:, CC + c, b:b + 1], X, xs)
                h = {}
                yield from layer_norm(X, xs["marks"], ada_at(7, b), ada_at(6, b), 1e-6, h)
                mlp_in[b] = h

        def mlp_chunk(h, n2, hid, hfree, marks):
            yield from held(gated_ring)
            gi, gated, gfree = gated_ring.take()
            for n in range(n2, n2 + 2):
                yield from held(bank_any, tanh_ring)
                bi, bank, bfree = bank_any.take()
                ti, th, tfree = tanh_ring.take()
                wait("pe", *h["marks"], W["m1"]["mark"], *bfree)
                project(bank[:, 0:L], W["m1"], slice(n * P, (n + 1) * P), h["pair"], CC, None)
                m = project(bank[:, L:2 * L], W["m1"], slice(HID + n * P, HID + (n + 1) * P), h["pair"],
                            CC, "pe_mlp")
                h["reads"] = [m]
                yield
                wait("act", m, *tfree)
                at = bias_at["m1"] + n
                t = act(th[:, 0, :], bank[:, 0:L], ACT.Tanh, "act_tanh", scale=0.5, bias=half_bias[:, n:n + 1])
                t = act(th[:, 1, :], bank[:, 0:L], ACT.Identity, "act_tanh", bias=bias_col[:, at:at + 1])
                yield
                wait("dve", t, *gfree)
                t = dve_stt(th[:, 0, :], th[:, 0, :], 1.0, th[:, 1, :], ALU.add, ALU.mult, "dve_mlp")
                yield
                wait("dve", t)
                t = dve_stt(gated[:, n - n2, :], bank[:, L:2 * L], bias_col[:, at + HC:at + HC + 1],
                            th[:, 0, :], ALU.add, ALU.mult, "dve_mlp")
                bank_any.release(bi, t)
                tanh_ring.release(ti, t)
            yield
            wait("act", t, *hfree)
            m1 = act(hid[:, 0, n2:n2 + 2, :], gated[:, :, :], ACT.Copy, "act_split")
            yield
            wait("pool", m1, *hfree)
            m2 = pool_tt(hid[:, 1, n2:n2 + 2, :], gated[:, :, :], hid[:, 0, n2:n2 + 2, :], ALU.subtract,
                         "pool_split")
            gated_ring.release(gi, m2)
            marks += [m1, m2]

        def mlp_part():
            for b in range(B):
                while b not in mlp_in:
                    yield
                xs, h = x_of[b], mlp_in[b]
                X = xs["tile"]
                yield from due(*h["marks"])
                yield from weights_ready(W["m2"])
                yield from held(hid_ring)
                hi_, hid, hfree = hid_ring.take()
                marks = []
                yield from together(*[mlp_chunk(h, n2, hid, hfree, marks) for n2 in range(0, HC, 2)])
                pair_ring.release(h["index"], *h["reads"])
                yield from due(*marks)
                yield from held(bank_any)
                bi, bank, bfree = bank_any.take()
                wait("pe", *marks, W["m2"]["mark"], *bfree)
                for c in range(CC):
                    m = project(bank[:, c * L:(c + 1) * L], W["m2"], slice(c * P, (c + 1) * P), hid, HC, "pe_mlp")
                hid_ring.release(hi_, m)
                yield
                yield from add_rows(bi, bank, m, lambda c, b=b: half_gate[:, c, b:b + 1],
                                    lambda c, b=b: gate_bias[:, 2 * CC + c, b:b + 1], X, xs)
                mlp_done[b] = True

        def last_keys_part():
            yield from modulated("ada_last")
            for b in range(B):
                while b not in top_slot:
                    yield
                yield from held(ctx_ring, last_k_parts)
                cm = {}
                load_context(b, cm)
                yield
                h, k, v = {}, {}, {}
                yield from layer_norm(cm["tile"], [cm["mark"]], ada_at(0, b, sskv), ada_at(1, b, sskv), 1e-5, h)
                ctx_ring.release(cm["index"], h["read"])
                yield from together(
                    project_parts(W["Wkv"], 0, bias_at_chunk(bias_at["bkv"]), h, last_k_parts, k),
                    project_values(W["Wkv"], C, h, values["soft"], v))
                pair_ring.release(h["index"], *h["reads"])
                last_keys[b] = k, v
                yield

        def last_query_part():
            yield from modulated("ada_last")
            for b in range(B):
                while b not in mlp_done:
                    yield
                yield from held(last_q_parts)
                xs = x_of[b]
                h, q = {}, {}
                yield from layer_norm(xs["tile"], xs["marks"], ada_at(0, b, ssq), ada_at(1, b, ssq), 1e-5, h)
                yield from project_parts(W["Wq"], 0, query_bias(2), h, last_q_parts, q)
                pair_ring.release(h["index"], *h["reads"])
                last_query[b] = q
                yield

        def last_part(first):
            for b in range(first, B, 2):
                while b not in last_keys or b not in last_query:
                    yield
                yield from held(stacks["soft"])
                ki, slot, _ = stacks["soft"].take()
                k, slot["v"] = last_keys[b]
                to_stack(slot, "k", k)
                to_stack(slot, "q", last_query[b])
                yield
                yield from held(osum_ring)
                oi, ot, ofree = osum_ring.take()
                osum = dict(index=oi, tile=ot, free=ofree)
                yield from attend(slot, False, osum)
                stacks["soft"].release(ki)
                last_osum[b] = osum

        def last_finish_part():
            for b in range(B):
                while b not in last_osum:
                    yield
                xs = x_of[b]
                X = xs["tile"]
                yield from finish_attention(last_osum[b], bias_at_chunk(bias_at["bkv"] + CC), W["Wp"], None,
                                            lambda c: bias_col[:, bias_at["bp"] + c:bias_at["bp"] + c + 1], X, xs)
                wait("sp", *xs["marks"])
                m = roll_copy(b, X, False, f"x_out{xs['index']}")
                X_ring.release(xs["index"], m)

        parts = prog.parts
        for part in (
                prologue(), top_part(), top_scores_part(), top_guard_part(), top_values_part(), load_part(),
                self_part(), window_part(0), window_part(1), top_keys_part(), query_part(), top_finish_part(),
                mlp_part(), last_keys_part(), last_query_part(), last_part(0), last_part(1),
                last_finish_part()):
            parts.append([0.0, part, False])
        idle = 0
        while parts:
            entry = min(parts, key=lambda e: e[0])
            prog.step_end, prog.now = 0.0, entry[0]
            try:
                next(entry[1])
            except StopIteration:
                parts.remove(entry)
                continue
            if prog.step_end == 0.0:
                entry[2] = True
                entry[0] = max(entry[0], min([e[0] for e in parts if not e[2]], default=entry[0])) + 10.0
                idle += 1
                assert idle < 2000, "no part can go on"
            else:
                entry[0], idle = prog.step_end, 0
                entry[2] = False
        for name, n in prog.count.items():
            if name[:3] in ("to_", "x_o"):
                wait("sp", (name, n))

        block = ctx.enter_context(nc.Block())

        @block.sync
        def _(eng):
            for f in prog.queue["sp"]:
                f(eng)

        @block.tensor
        def _(eng):
            for f in prog.queue["pe"]:
                f(eng)

        @block.scalar
        def _(eng):
            for f in prog.queue["act"]:
                f(eng)

        @block.vector
        def _(eng):
            for f in prog.queue["dve"]:
                f(eng)

        @block.gpsimd
        def _(eng):
            for f in prog.queue["pool"]:
                f(eng)


def kernel(**inputs):
    import numpy as np
    import concourse.bacc as bacc
    from concourse.bass_utils import run_bass_kernel_spmd

    nc = bacc.Bacc("TRN2", target_bir_lowering=False, num_devices=1)
    arrays, aps = {}, {}
    for name, value in inputs.items():
        a = np.ascontiguousarray(value)
        arrays[f"in_{name}"] = a
        aps[name] = nc.dram_tensor(f"in_{name}", a.shape, mybir.dt.from_np(a.dtype), kind="ExternalInput").ap()
    shape = inputs["x"].shape
    out = nc.dram_tensor("out_x", shape, F32, kind="ExternalOutput").ap()
    build(nc, aps, out)
    r = run_bass_kernel_spmd(nc, [arrays], core_ids=[0])
    return r.results[0]["out_x"]
```
